# Optimizing a Trainium2 kernel written in Bass

```python
import numpy as np
import jax
import jax.numpy as jnp

def _softmax(x, axis=-1):
    return jax.nn.softmax(x, axis=axis)

def _gelu(x):
    return jax.nn.gelu(x, approximate=True)

def _silu(x):
    return jax.nn.silu(x)

def _sigmoid(x):
    return jax.nn.sigmoid(x)

def _layernorm(x, axis=-1, eps=1e-05):
    m = jnp.mean(x, axis=axis, keepdims=True)
    v = jnp.var(x, axis=axis, keepdims=True)
    return (x - m) / jnp.sqrt(v + eps)

def _scatter_add(tgt, idx, src, axis=0):
    return tgt.at[idx].add(src)

def _segment_sum(src, seg, n):
    return jax.ops.segment_sum(src, seg, n)
kernel_name = 'mk_macaron_d1_jaxref_r8_a850a0'

def setup_inputs(seed: int=0):
    np.random.seed(seed)
    _w = jnp.asarray

    def _L0_attn_setup():
        import jax, jax.numpy as jnp
        import numpy as np
        D_MODEL = 128
        NUM_HEADS = 16
        HEAD_DIM = D_MODEL // NUM_HEADS
        ALPHA = 1.0
        key = jax.random.key(seed)
        ks = jax.random.split(key, 9)
        B, T, D = (2, 256, D_MODEL)
        s = 1.0 / np.sqrt(D)
        inp = {'x': jax.random.normal(ks[0], (B, T, D), dtype=jnp.float32), 'Wq': jax.random.uniform(ks[1], (D, D), jnp.float32, -s, s), 'bq': jax.random.uniform(ks[2], (D,), jnp.float32, -s, s), 'Wk': jax.random.uniform(ks[3], (D, D), jnp.float32, -s, s), 'bk': jax.random.uniform(ks[4], (D,), jnp.float32, -s, s), 'Wv': jax.random.uniform(ks[5], (D, D), jnp.float32, -s, s), 'bv': jax.random.uniform(ks[6], (D,), jnp.float32, -s, s), 'Wo': jax.random.uniform(ks[7], (D, D), jnp.float32, -s, s), 'bo': jax.random.uniform(ks[8], (D,), jnp.float32, -s, s)}
        return inp
    _L0_attn_in = _L0_attn_setup()

    def _L0_ffn_setup():
        import jax, jax.numpy as jnp
        import numpy as np
        B, T, D, E, K = (2, 256, 128, 8, 2)
        H = 2 * D
        key = jax.random.key(seed)
        ks = jax.random.split(key, 5)
        s = 0.02
        return {'x': jax.random.normal(ks[0], (B, T, D), jnp.float32), 'Wr': jax.random.normal(ks[1], (D, E), jnp.float32) * s, 'br': jnp.zeros((E,), jnp.float32), 'W1': jax.random.normal(ks[2], (E, D, H), jnp.float32) * s, 'b1': jnp.zeros((E, H), jnp.float32), 'W2': jax.random.normal(ks[3], (E, H, D), jnp.float32) * s, 'b2': jnp.zeros((E, D), jnp.float32)}
    _L0_ffn_in = _L0_ffn_setup()
    _d = {'L0_attn_x': _L0_attn_in['x'], 'L0_attn_Wq': _L0_attn_in['Wq'], 'L0_attn_bq': _L0_attn_in['bq'], 'L0_attn_Wk': _L0_attn_in['Wk'], 'L0_attn_bk': _L0_attn_in['bk'], 'L0_attn_Wv': _L0_attn_in['Wv'], 'L0_attn_bv': _L0_attn_in['bv'], 'L0_attn_Wo': _L0_attn_in['Wo'], 'L0_attn_bo': _L0_attn_in['bo'], 'L0_ffn_Wr': _L0_ffn_in['Wr'], 'L0_ffn_br': _L0_ffn_in['br'], 'L0_ffn_W1': _L0_ffn_in['W1'], 'L0_ffn_b1': _L0_ffn_in['b1'], 'L0_ffn_W2': _L0_ffn_in['W2'], 'L0_ffn_b2': _L0_ffn_in['b2']}
    _x0 = _d['L0_attn_x']
    _d['L0_attn_x'] = jax.random.normal(jax.random.fold_in(jax.random.key(seed), 1), (32, 256, 128), dtype=_x0.dtype)
    del _x0
    return _d

def reference(L0_attn_x, L0_attn_Wq, L0_attn_bq, L0_attn_Wk, L0_attn_bk, L0_attn_Wv, L0_attn_bv, L0_attn_Wo, L0_attn_bo, L0_ffn_Wr, L0_ffn_br, L0_ffn_W1, L0_ffn_b1, L0_ffn_W2, L0_ffn_b2):

    def _L0_attn_ref(x, Wq, bq, Wk, bk, Wv, bv, Wo, bo):
        import jax, jax.numpy as jnp
        import numpy as np
        D_MODEL = 128
        NUM_HEADS = 16
        HEAD_DIM = D_MODEL // NUM_HEADS
        ALPHA = 1.0
        B, T, D = x.shape
        H, hd = (NUM_HEADS, HEAD_DIM)

        def split_heads(y):
            return y.reshape(B, T, H, hd).transpose(0, 2, 1, 3)
        Q = split_heads(x @ Wq.T + bq)
        K = split_heads(x @ Wk.T + bk)
        V = split_heads(x @ Wv.T + bv)
        scores = jnp.einsum('bhid,bhjd->bhij', Q, K) / jnp.sqrt(jnp.float32(hd))
        t = jnp.arange(T)
        delta = t[:, None] - t[None, :]
        causal_mask = delta < 0
        decay = jnp.where(causal_mask, 0.0, -delta.astype(jnp.float32) ** ALPHA)
        scores = jnp.where(causal_mask, -jnp.inf, scores) + decay
        attn = jax.nn.softmax(scores, axis=-1)
        out = jnp.einsum('bhij,bhjd->bhid', attn, V)
        out = out.transpose(0, 2, 1, 3).reshape(B, T, D)
        return out @ Wo.T + bo

    def _L0_ffn_ref(x, Wr, br, W1, b1, W2, b2):
        import jax, jax.numpy as jnp
        import numpy as np
        B, T, D, E, K = (2, 256, 128, 8, 2)
        H = 2 * D
        logits = jnp.einsum('btd,de->bte', x, Wr) + br
        topv, topi = jax.lax.top_k(logits, K)
        sel_mask = jax.nn.one_hot(topi, E, dtype=logits.dtype).sum(-2) > 0
        neg_inf = jnp.finfo(logits.dtype).min
        gates = jax.nn.softmax(jnp.where(sel_mask, logits, neg_inf), axis=-1)
        h = jax.nn.relu(jnp.einsum('btd,edh->bteh', x, W1) + b1)
        out = jnp.einsum('bte,bteh,ehd->btd', gates, h, W2)
        out = out + jnp.einsum('bte,ed->btd', gates, b2)
        return out
    x = L0_attn_x
    x = x + 0.5 * _L0_ffn_ref(_layernorm(x, axis=-1), L0_ffn_Wr, L0_ffn_br, L0_ffn_W1, L0_ffn_b1, L0_ffn_W2, L0_ffn_b2)
    x = x + _L0_attn_ref(_layernorm(x, axis=-1), L0_attn_Wq, L0_attn_bq, L0_attn_Wk, L0_attn_bk, L0_attn_Wv, L0_attn_bv, L0_attn_Wo, L0_attn_bo)
    x = x + 0.5 * _L0_ffn_ref(_layernorm(x, axis=-1), L0_ffn_Wr, L0_ffn_br, L0_ffn_W1, L0_ffn_b1, L0_ffn_W2, L0_ffn_b2)
    return x

_drawn_inputs = setup_inputs


def setup_inputs(seed=0):
    import zlib

    import numpy as np

    out = dict(_drawn_inputs(seed))
    spreads = {'L0_ffn_br': (0.0, 0.1), 'L0_ffn_b1': (0.0, 0.555), 'L0_ffn_b2': (0.0, 0.1)}
    factors = {'L0_attn_bq': 8.0, 'L0_attn_bk': 8.0}
    for name, (base, spread) in spreads.items():
        noise = np.random.default_rng([zlib.crc32(name.encode()), seed]).standard_normal(out[name].shape)
        drawn = base * np.exp(spread * noise) if base else spread * noise
        out[name] = jnp.asarray(drawn.astype(out[name].dtype))
    for name, factor in factors.items():
        out[name] = (out[name] * factor).astype(out[name].dtype)
    return out
```

```python
import concourse.bass as bass
from concourse import mybir
from contextlib import ExitStack

F32 = mybir.dt.float32
F32R = mybir.dt.float32r
BF16 = mybir.dt.bfloat16
ALU = mybir.AluOpType
ACT = mybir.ActivationFunctionType
AX = mybir.AxisListType

P = 128
D = 128
T = 256
B = 32
CH = 512
TT = CH // P
NC = B * T // CH
H, HD = 16, 8
E, HID = 8, 256
EPS = 1e-5
QSCALE = 1.0 / float(HD) ** 0.5
PIECES = 6
ROWS_QK = PIECES * HD
ROWS_A = ROWS_QK + 2
ROWS_B = ROWS_A + 3
HSLOT = 16

LOOP_FROM, LOOP_TO = 2, 14


def call_ff1(k):
    return k if k < 2 else 2 * k - 2


def call_ff2(k):
    return 2 * k + 3 if k < NC - 2 else 16 + k


def steps(c):
    def there(k):
        return 0 <= k < NC

    att_b = {19: [0], 20: [1], 21: [2], 22: [3, 4], 23: [5], 24: [6], 25: [7, 8], 26: [9], 27: [10],
             28: [11, 12], 29: [13], 30: [14], 31: [15]}
    out = []
    if there(c + 2) and c + 2 >= 2:
        out.append(("load_x", c + 2))
    for k in range(32):
        if k < HSLOT and there(c + 1):
            out.append(("up", 1, c + 1, k))
        if k >= HSLOT and there(c - 1):
            out.append(("up", 2, c - 1, k - HSLOT))
        if there(c) and k < H:
            out.append(("score_max", c, k))
        if there(c) and k in att_b:
            out.append(("score_exp", c, att_b[k][0]))
        if k < 2 and there(c - 2):
            out.append(("down", 2, c - 2, 14 + k))
        if 2 <= k < 18 and there(c + 1):
            out.append(("down", 1, c + 1, k - 2))
        if k >= 18 and there(c - 1):
            out.append(("down", 2, c - 1, k - 18))
        if k == 2 and there(c - 2):
            out.append(("store", c - 2))
        if there(c) and k in att_b and len(att_b[k]) > 1:
            out.append(("score_exp", c, att_b[k][1]))
        if there(c) and k in (24, 27, 30):
            out.append(("pv", c, (k - 24) // 3))
        if there(c - 1):
            if k == 1:
                out.append(("pv", c - 1, 3))
                out.append(("seed_x2", c - 1))
            if 3 <= k <= 6:
                out.append(("normalise", c - 1, k - 3))
            if k == 7:
                out.append(("transpose_o", c - 1))
            if k == 8:
                out.append(("project_o", c - 1))
                out.append(("ln", 2, c - 1))
            if k == 10:
                out.append(("transpose_x", 2, c - 1))
            if k == 11:
                out.append(("route", 2, c - 1))
            if k == 13:
                out.append(("transpose_g", 2, c - 1))
            if k == 14:
                out.append(("bias_down", 2, c - 1))
        if there(c) and k == 16:
            out.append(("send_max", c))
        if there(c + 1):
            if k == 18:
                out.append(("ln", 0, c + 1))
            if k == 20:
                out.append(("transpose_x", 0, c + 1))
            if k == 21:
                out.append(("project_q", c + 1))
            if k == 22:
                out.append(("project_k", c + 1))
            if k == 23:
                out.append(("project_v", c + 1))
        if there(c + 2):
            if k == 24:
                out.append(("ln", 1, c + 2))
            if k == 26:
                out.append(("transpose_x", 1, c + 2))
            if k == 27:
                out.append(("route", 1, c + 2))
            if k == 29:
                out.append(("transpose_g", 1, c + 2))
            if k == 30:
                out.append(("bias_down", 1, c + 2))
    return out


SHARED = ("normalise", "transpose_o", "project_o", "transpose_x", "route", "transpose_g", "bias_down",
          "send_max", "project_q", "project_k", "project_v")
SHARED_AT = {s: n for n, s in enumerate(s for c in range(-2, NC + 2) for s in steps(c) if s[0] in SHARED)}


def macaron_kernel(nc, x, wq, bq, wk, bk, wv, bv, wo, bo, wr, br, w1, b1, w2, b2,
                   ident, ident_b, mask_b, tri, qrows, krows, zq, zk, out):
    x_v = x.rearrange("(c t p) d -> c p t d", t=TT, p=P)
    out_v = out.rearrange("(c t p) d -> c p t d", t=TT, p=P)

    with ExitStack() as ctx:
        def sb(name, shape, dt=F32):
            return ctx.enter_context(nc.sbuf_tensor(name, shape, dt))

        def sem(name):
            return ctx.enter_context(nc.semaphore(name))

        w1_f = sb("w1_f", [P, E * HID])
        w1_hi = sb("w1_hi", [P, E * HID], F32R)
        w1_lo = sb("w1_lo", [P, E * HID], F32R)
        w2_sb = sb("w2_sb", [P, E, 2, D])
        b1_sb = sb("b1_sb", [P, E * 2])
        b2_sb = sb("b2_sb", [E, D])
        wr_sb = sb("wr_sb", [P, E])
        br_bc = sb("br_bc", [P, E])
        wqk_f = sb("wqk_f", [P, 2, D])
        wqk_hi = sb("wqk_hi", [P, 2, D], F32R)
        wqk_lo = sb("wqk_lo", [P, 2, D], F32R)
        wv_sb = sb("wv_sb", [P, D])
        wo_sb = sb("wo_sb", [P, D])
        bq_sb = sb("bq_sb", [P, 1])
        bqs_sb = sb("bqs_sb", [P, 1])
        bk_sb = sb("bk_sb", [P, 1])
        bv_bc = sb("bv_bc", [P, D])
        bo_bc = sb("bo_bc", [P, D])
        id_f = sb("id_f", [P, P])
        id_b = sb("id_b", [P, P], BF16)
        mask_sb = sb("mask_sb", [P, P], BF16)
        tri_sb = sb("tri_sb", [P, E, E])
        minus_half = sb("minus_half", [P, TT])
        x_in = sb("x_in", [P, 2, TT, D])
        x1 = sb("x1", [P, 2, TT, D])
        x2 = sb("x2", [P, 2, TT, D])
        y_out = sb("y_out", [P, 2, TT, D])
        stats = sb("stats", [P, 2, TT, 6])
        mv = sb("mv", [P, 2, TT, 2])
        var_eps = sb("var_eps", [P, 2, TT])
        rstd = sb("rstd", [P, 2, TT])
        xn = sb("xn", [P, 2, TT, D])
        xt = sb("xt", [P, 2, CH])
        xa_hi = sb("xa_hi", [P, CH], F32R)
        xa_lo = sb("xa_lo", [P, CH], F32R)
        xf_hi = sb("xf_hi", [P, 2, CH], F32R)
        xf_lo = sb("xf_lo", [P, 2, CH], F32R)
        logit = sb("logit", [P, TT, E])
        top = sb("top", [P, TT])
        below = sb("below", [P, TT, E])
        expd = sb("expd", [P, TT, E])
        beats = sb("beats", [P, TT, E, E])
        ties = sb("ties", [P, TT, E, E])
        rank = sb("rank", [P, TT, E])
        chosen = sb("chosen", [P, TT, E])
        gsum = sb("gsum", [P, TT])
        grec = sb("grec", [P, TT])
        gates = sb("gates", [P, 2, TT, E])
        gates_t = sb("gates_t", [E, CH])
        hid = sb("hid", [P, 4, CH])
        q_f = sb("q_f", [P, CH])
        k_f = sb("k_f", [P, CH])
        q_rest = sb("q_rest", [P, CH])
        k_rest = sb("k_rest", [P, CH])
        q_part = sb("q_part", [P, 3, CH], BF16)
        k_part = sb("k_part", [P, 3, CH], BF16)
        q_st = [sb(f"q_st{i}", [P, H // 2, CH], BF16) for i in range(2)]
        k_st = [sb(f"k_st{i}", [P, H // 2, CH], BF16) for i in range(2)]
        v_st = [sb(f"v_st{i}", [P, TT, H, 32]) for i in range(2)]
        mx = sb("mx", [P, TT, H])
        neg_mx = sb("neg_mx", [P, TT, 2, H // 2])
        mx_rest = sb("mx_rest", [P, TT * H])
        mx_part = sb("mx_part", [P, TT, 3, H], BF16)
        mx_t = sb("mx_t", [3 * H, CH], BF16)
        prob = sb("prob", [P, 8, 2, 3, P])
        o_t = sb("o_t", [P, 4, CH])
        o_rec = sb("o_rec", [P, H])
        o_n = sb("o_n", [P, TT, D])
        o_nt = sb("o_nt", [P, CH])

        up_ps = ctx.enter_context(nc.psum_tensor("up_ps", [P, 2, CH], F32))
        down_ps = ctx.enter_context(nc.psum_tensor("down_ps", [P, 2, TT, D], F32))
        score_ps = ctx.enter_context(nc.psum_tensor("score_ps", [P, 2, CH], F32))
        o_ps = ctx.enter_context(nc.psum_tensor("o_ps", [P, CH], F32))
        shared_ps = ctx.enter_context(nc.psum_tensor("shared_ps", [P, CH], F32))
        shared_bf = shared_ps[:, :].bitcast(BF16)

        loaded = sem("loaded")
        weights_split = sem("weights_split")
        cleared = sem("cleared")
        x_loaded = [sem(f"x_loaded{i}") for i in range(2)]
        out_stored = [sem(f"out_stored{i}") for i in range(2)]
        up_filled = sem("up_filled")
        up_relued = sem("up_relued")
        down_filled = sem("down_filled")
        down_added = sem("down_added")
        stats_done = [sem(f"stats_done{i}") for i in range(2)]
        moments_done = [sem(f"moments_done{i}") for i in range(2)]
        var_done = [sem(f"var_done{i}") for i in range(2)]
        rstd_done = [sem(f"rstd_done{i}") for i in range(2)]
        xn_done = [sem(f"xn_done{i}") for i in range(2)]
        xsplit = [sem(f"xsplit{i}") for i in range(2)]
        shared_filled = sem("shared_filled")
        shared_emptied = sem("shared_emptied")
        gate_step = sem("gate_step")
        gates_done = sem("gates_done")
        gate_exp = sem("gate_exp")
        qsplit = sem("qsplit")
        ksplit = sem("ksplit")
        qk_out = sem("qk_out")
        qk_in = sem("qk_in")
        max_filled = sem("max_filled")
        max_taken = sem("max_taken")
        max_step = sem("max_step")
        max_in = sem("max_in")
        exp_filled = sem("exp_filled")
        exp_done = sem("exp_done")
        pv_filled = sem("pv_filled")
        o_copied = sem("o_copied")
        rec_done = sem("rec_done")
        held = sem("held")
        x2_seeded = sem("x2_seeded")

        LOADS = 26
        GATE_STEPS, SPLIT_STEPS, MAX_STEPS = 10, 4, 5

        block = ctx.enter_context(nc.Block())

        class Phase:

            def __init__(self, c, i=None):
                self.c, self.i = c, i

            def count(self, f):
                if self.i is None:
                    return f(0)
                return f(0) + self.i * (f(2) - f(0))

        def phases(eng, body):
            for c in range(-2, LOOP_FROM):
                body(Phase(c))
            with eng.Fori(0, (LOOP_TO - LOOP_FROM) // 2) as i:
                for c in range(LOOP_FROM, LOOP_FROM + 2):
                    body(Phase(c, i))
            for c in range(LOOP_TO, NC + 2):
                body(Phase(c))

        def shared_count(ph, s):
            def f(o):
                at = s[:-1] + (s[-1] + o,) if s[0] in ("transpose_x", "route", "transpose_g", "bias_down", "transpose_o",
                                                       "project_o", "send_max", "project_q", "project_k",
                                                       "project_v") else (s[0], s[1] + o, s[2])
                return SHARED_AT[at] + 1
            return ph.count(f)

        def call(which, k):
            return call_ff1(k) if which == 1 else call_ff2(k)

        def hold(eng):
            eng.sem_inc(held, 1)

        def ln_count(ph, which, k, per):
            return ph.count(lambda o: per * (k + o if which == 0 else call(which, k + o)))

        @block.sync
        def _(sp):
            for dst, src in ((w1_f[:, :], w1), (w2_sb[:, :, :, :], w2), (b1_sb[:, :], b1), (b2_sb[:, :], b2),
                             (wr_sb[:, :], wr), (br_bc[:, :], br.partition_broadcast(P)),
                             (wqk_f[:, 0, :], wq), (wqk_f[:, 1, :], wk), (wv_sb[:, :], wv), (wo_sb[:, :], wo),
                             (bq_sb[:, :], bq), (bk_sb[:, :], bk), (bv_bc[:, :], bv.partition_broadcast(P)),
                             (bo_bc[:, :], bo.partition_broadcast(P)), (id_f[:, :], ident), (id_b[:, :], ident_b),
                             (mask_sb[:, :], mask_b), (tri_sb[:, :, :].rearrange("p e f -> p (e f)"),
                                                       tri.partition_broadcast(P))):
                sp.dma_start(dst, src).then_inc(loaded, 16)
            for st, rows in ((q_st, qrows), (k_st, krows)):
                sp.dma_start(st[0][ROWS_QK:64, :, :], rows).then_inc(loaded, 16)
            for st, rows in ((q_st, qrows), (k_st, krows)):
                for i, a in ((0, 1), (1, 0), (1, 1)):
                    sp.dma_start(st[i][64 * a + ROWS_QK:64 * a + 64, :, :], rows).then_inc(loaded, 16)
            for k in range(2):
                sp.dma_start(x_in[:, k, :, :], x_v[k]).then_inc(x_loaded[k], 16)

            def body(ph):
                for s in steps(ph.c):
                    if s[0] == "load_x":
                        k = s[1]
                        sp.wait_ge(shared_emptied, shared_count(ph, ("bias_down", 1, k - 2)))
                        hold(sp)
                        sp.dma_start(x_in[:, k % 2, :, :], x_v[ph.count(lambda o: k + o)])\
                            .then_inc(x_loaded[k % 2], 16)
                    if s[0] == "store":
                        k = s[1]
                        sp.wait_ge(down_added, ph.count(lambda o: 16 * call_ff2(k + o) + 16))
                        hold(sp)
                        sp.dma_start(out_v[ph.count(lambda o: k + o)], y_out[:, k % 2, :, :])\
                            .then_inc(out_stored[k % 2], 16)
                    if s[0] == "send_max":
                        c = s[1]
                        sp.wait_ge(shared_emptied, shared_count(ph, s))
                        hold(sp)
                        for a in range(2):
                            for piece in range(3):
                                row = 64 * a + ROWS_A + piece
                                src = piece * H + a * (H // 2)
                                sp.dma_start(q_st[c % 2][row:row + 1, :, :], mx_t[src:src + H // 2, :])\
                                    .then_inc(max_in, 16)
                    if s[0] == "project_v":
                        c = s[1]
                        sp.wait_ge(qsplit, ph.count(lambda o: SPLIT_STEPS * (c + o + 1)))
                        hold(sp)
                        for z, part, dup in ((zq, q_part, False), (zk, k_part, True)):
                            if dup:
                                sp.wait_ge(ksplit, ph.count(lambda o: SPLIT_STEPS * (c + o + 1)))
                                hold(sp)
                                src = (part[:, 0:1, :].broadcast_to([P, 3, CH]),
                                       part[:, 1:2, :].broadcast_to([P, 2, CH]), part[:, 2:3, :])
                            else:
                                src = (part[:, 0:3, :], part[:, 0:2, :], part[:, 0:1, :])
                            for (r0, r1), sr in zip(((0, 3), (3, 5), (5, 6)), src):
                                sp.dma_start(z[c % 2, :, r0:r1, :], sr).then_inc(qk_out, 16)
                        sp.wait_ge(qk_out, ph.count(lambda o: 96 * (c + o + 1)))
                        hold(sp)
                        if c >= 2:
                            sp.wait_ge(exp_filled, ph.count(lambda o: H * (c + o - 1)))
                            hold(sp)
                        for z, st in ((zq, q_st), (zk, k_st)):
                            zr = z[c % 2].rearrange("(t a d) r n -> a (d r) t n", a=2, d=HD)
                            for a in range(2):
                                sp.dma_start(st[c % 2][64 * a:64 * a + ROWS_QK, :, :], zr[a]).then_inc(qk_in, 16)

            phases(sp, body)
            for k in range(2):
                sp.wait_ge(out_stored[k], 16 * NC // 2)

        @block.gpsimd
        def _(pool):
            for st in v_st:
                nc.gpsimd.memset(st[:, :, :, :], 0.0)
            nc.gpsimd.memset(minus_half[:, :], -0.5).then_inc(cleared, 1)
            pool.wait_ge(cleared, 1)
            for st in v_st:
                last = nc.gpsimd.memset(st[:, :, :, HD:HD + 1], 1.0)
            last.then_inc(cleared, 1)
            pool.wait_ge(loaded, 16 * LOADS)

            def body(ph):
                for s in steps(ph.c):
                    if s[0] == "ln":
                        which, k = s[1], s[2]
                        m = min(which, 1)
                        pool.wait_ge(moments_done[m], ln_count(ph, which, k, TT) + TT)
                        hold(pool)
                        nc.gpsimd.tensor_scalar(var_eps[:, m, :], mv[:, m, :, 1], EPS, None, ALU.add)\
                            .then_inc(var_done[m], 1)
                        pool.wait_ge(var_done[m], ln_count(ph, which, k, 1) + 1)
                        nc.gpsimd.tensor_tensor(rstd[:, m, :], var_eps[:, m, :], minus_half[:, :], ALU.pow)\
                            .then_inc(rstd_done[m], 1)
                    if s[0] == "seed_x2":
                        c = s[1]
                        pool.wait_ge(down_added, ph.count(lambda o: 16 * call_ff1(c + o) + 16))
                        if c >= 2:
                            pool.wait_ge(shared_emptied, shared_count(ph, ("bias_down", 2, c - 2)))
                        nc.gpsimd.tensor_tensor(x2[:, c % 2, :, :], x1[:, c % 2, :, :],
                                                bo_bc[:, :].unsqueeze(1).broadcast_to([P, TT, D]), ALU.add)\
                            .then_inc(x2_seeded, 1)
                    if s[0] == "project_k":
                        c = s[1]

                        def step(n):
                            return ph.count(lambda o: SPLIT_STEPS * (c + o) + n)

                        pool.wait_ge(shared_emptied, shared_count(ph, s))
                        if c >= 1:
                            pool.wait_ge(qk_out, ph.count(lambda o: 96 * (c + o)))
                        hold(pool)
                        nc.gpsimd.tensor_copy(k_part[:, 0, :], k_f[:, :]).then_inc(ksplit, 1)
                        pool.wait_ge(ksplit, step(1))
                        nc.gpsimd.tensor_tensor(k_rest[:, :], k_f[:, :], k_part[:, 0, :], ALU.subtract)\
                            .then_inc(ksplit, 1)
                        pool.wait_ge(ksplit, step(2))
                        hold(pool)
                        nc.gpsimd.tensor_copy(k_part[:, 1, :], k_rest[:, :]).then_inc(ksplit, 1)
                        pool.wait_ge(ksplit, step(3))
                        nc.gpsimd.tensor_tensor(k_part[:, 2, :], k_rest[:, :], k_part[:, 1, :], ALU.subtract)\
                            .then_inc(ksplit, 1)

            phases(pool, body)

        @block.scalar
        def _(act):
            act.wait_ge(loaded, 16 * LOADS)
            act.wait_ge(weights_split, 5)

            def body(ph):
                for s in steps(ph.c):
                    if s[0] == "up":
                        which, k, t = s[1:]
                        tile = ph.count(lambda o: HSLOT * call(which, k + o) + t)
                        act.wait_ge(up_filled, tile + 1)
                        if HSLOT * call(which, k) + t >= 4:
                            act.wait_ge(down_filled, tile - t % 2 - 2)
                        nc.scalar.activation(hid[:, t % 4, :], up_ps[:, t % 2, :], ACT.Relu,
                                             bias=b1_sb[:, t:t + 1]).then_inc(up_relued, 1)
                    if s[0] == "score_exp":
                        c, h = s[1], s[2]
                        act.wait_ge(exp_filled, ph.count(lambda o: H * (c + o) + h + 1))
                        if h % 4 == 0 and 4 * c + h // 4 >= 2:
                            act.wait_ge(pv_filled, ph.count(lambda o: 4 * (c + o) + h // 4 - 1))
                        nc.scalar.activation(prob[:, h % 8, :, :, :].rearrange("p b s n -> p b (s n)"),
                                             score_ps[:, :, 0:3 * P], ACT.Exp).then_inc(exp_done, 1)
                    if s[0] == "pv":
                        c, g = s[1], s[2]
                        act.wait_ge(pv_filled, ph.count(lambda o: 4 * (c + o) + g + 1))
                        if c >= 1 and g == 0:
                            act.wait_ge(shared_filled, shared_count(ph, ("normalise", c - 1, 3)))
                        nc.scalar.activation(o_t[:, g, :], o_ps[:, :], ACT.Copy).then_inc(o_copied, 1)
                    if s[0] == "transpose_x":
                        which, k = s[1], s[2]
                        m = min(which, 1)
                        act.wait_ge(shared_filled, shared_count(ph, s))
                        if which == 0:
                            if k >= 1:
                                act.wait_ge(xsplit[0], ph.count(lambda o: 2 * (k + o)))
                        elif call(which, k) >= 1:
                            act.wait_ge(xsplit[1], ph.count(lambda o: 2 * call(which, k + o)))
                        nc.scalar.activation(xt[:, m, :], shared_ps[:, :], ACT.Copy).then_inc(shared_emptied, 1)
                    if s[0] == "route":
                        which, k = s[1], s[2]
                        act.wait_ge(gate_step, ph.count(lambda o: GATE_STEPS * call(which, k + o) + 2))
                        nc.scalar.activation(expd[:, :, :], below[:, :, :], ACT.Exp).then_inc(gate_exp, 1)
                    if s[0] == "transpose_g":
                        act.wait_ge(shared_filled, shared_count(ph, s))
                        nc.scalar.activation(gates_t[:, :], shared_ps[0:E, :], ACT.Copy).then_inc(shared_emptied, 1)
                    if s[0] == "project_q":
                        c = s[1]
                        act.wait_ge(shared_filled, shared_count(ph, s))
                        if c >= 1:
                            act.wait_ge(qsplit, ph.count(lambda o: SPLIT_STEPS * (c + o)))
                        nc.scalar.activation(q_f[:, :], shared_ps[:, :], ACT.Identity, bias=bqs_sb[:, 0:1],
                                             scale=QSCALE).then_inc(shared_emptied, 1)
                    if s[0] == "project_k":
                        c = s[1]
                        act.wait_ge(shared_filled, shared_count(ph, s))
                        if c >= 1:
                            act.wait_ge(ksplit, ph.count(lambda o: SPLIT_STEPS * (c + o)))
                        nc.scalar.activation(k_f[:, :], shared_ps[:, :], ACT.Identity, bias=bk_sb[:, 0:1])\
                            .then_inc(shared_emptied, 1)
                    if s[0] == "send_max":
                        c = s[1]
                        act.wait_ge(shared_filled, shared_count(ph, s))
                        if c >= 1:
                            act.wait_ge(max_in, ph.count(lambda o: 96 * (c + o)))
                        nc.scalar.activation(mx_t[:, :], shared_bf[0:3 * H, 0:CH], ACT.Copy)\
                            .then_inc(shared_emptied, 1)
                    if s[0] == "transpose_o":
                        act.wait_ge(shared_filled, shared_count(ph, s))
                        nc.scalar.activation(o_nt[:, :], shared_ps[:, :], ACT.Copy).then_inc(shared_emptied, 1)

            phases(act, body)

        @block.vector
        def _(dve):
            dve.wait_ge(loaded, 16 * LOADS)
            w1_hi_f, w1_hi_r = w1_hi[:, :].bitcast(F32), w1_hi[:, :]
            nc.vector.tensor_copy(w1_hi_r, w1_f[:, :]).then_inc(weights_split, 1)
            nc.vector.tensor_copy(wqk_hi[:, :, :], wqk_f[:, :, :]).then_inc(weights_split, 1)
            nc.vector.tensor_scalar(bqs_sb[:, :], bq_sb[:, :], QSCALE, None, ALU.mult).then_inc(weights_split, 1)
            dve.wait_ge(weights_split, 2)
            nc.vector.tensor_tensor(w1_lo[:, :], w1_f[:, :], w1_hi_f, ALU.subtract).then_inc(weights_split, 1)
            nc.vector.tensor_tensor(wqk_lo[:, :, :], wqk_f[:, :, :], wqk_hi[:, :, :].bitcast(F32), ALU.subtract)\
                .then_inc(weights_split, 1)

            def body(ph):
                for s in steps(ph.c):
                    if s[0] == "down":
                        which, k, t = s[1:]
                        e, half = t // 2, t % 2
                        n = call(which, k)
                        acc = x1 if which == 1 else y_out
                        at = ph.count(lambda o: HSLOT * call(which, k + o) + t)
                        dve.wait_ge(down_filled, at + 1)
                        if e >= 1:
                            dve.wait_ge(down_added, at - 1)
                        elif half == 0:
                            dve.wait_ge(shared_emptied, shared_count(ph, ("bias_down", which, k)))
                        for tt in (2 * half, 2 * half + 1):
                            last = nc.vector.scalar_tensor_tensor(
                                out=acc[:, k % 2, tt, :], in0=down_ps[:, half, tt % 2, :],
                                scalar=gates[:, n % 2, tt, e:e + 1], in1=acc[:, k % 2, tt, :],
                                op0=ALU.mult, op1=ALU.add)
                        last.then_inc(down_added, 1)
                    if s[0] == "ln":
                        which, k = s[1], s[2]
                        m = min(which, 1)
                        src = (x1, x_in, x2)[which]
                        if which == 0:
                            dve.wait_ge(down_added, ph.count(lambda o: 16 * call_ff1(k + o) + 16))
                        elif which == 1:
                            dve.wait_ge(x_loaded[k % 2], ph.count(lambda o: 16 * ((k + o) // 2 + 1)))
                        else:
                            dve.wait_ge(shared_emptied, shared_count(ph, ("project_o", k)))
                        for tt in range(TT):
                            nc.vector.bn_stats(stats[:, m, tt, :], src[:, k % 2, tt, :]).then_inc(stats_done[m], 1)
                        dve.wait_ge(stats_done[m], ln_count(ph, which, k, TT) + TT)
                        first = k == 0 and which < 2
                        if not first:
                            dve.wait_ge(rstd_done[m], ln_count(ph, which, k, 1))
                        hold(dve)
                        for tt in range(TT):
                            nc.vector.bn_aggr(mv[:, m, tt, :], stats[:, m, tt, :]).then_inc(moments_done[m], 1)
                        dve.wait_ge(rstd_done[m], ln_count(ph, which, k, 1) + 1)
                        dve.wait_ge(moments_done[m], ln_count(ph, which, k, TT) + TT)
                        if which == 0 and k >= 1:
                            dve.wait_ge(shared_filled, shared_count(ph, ("transpose_x", 0, k - 1)))
                        elif which > 0 and not first:
                            dve.wait_ge(xsplit[1], ph.count(lambda o: 2 * call(which, k + o)))
                        for tt in range(TT):
                            nc.vector.tensor_scalar(xn[:, m, tt, :], src[:, k % 2, tt, :], mv[:, m, tt, 0:1],
                                                    rstd[:, m, tt:tt + 1], ALU.subtract, ALU.mult)\
                                .then_inc(xn_done[m], 1)
                    if s[0] == "transpose_x":
                        which, k = s[1], s[2]
                        m = min(which, 1)
                        dve.wait_ge(shared_emptied, shared_count(ph, s))
                        if which == 0:
                            hi, lo = xa_hi[:, :], xa_lo[:, :]
                            if k >= 1:
                                dve.wait_ge(shared_filled, shared_count(ph, ("project_k", k - 1)))
                        else:
                            n = call(which, k)
                            hi, lo = xf_hi[:, n % 2, :], xf_lo[:, n % 2, :]
                            if n >= 2:
                                dve.wait_ge(up_filled, ph.count(lambda o: HSLOT * (call(which, k + o) - 1)))
                        nc.vector.tensor_copy(hi, xt[:, m, :]).then_inc(xsplit[m], 1)
                        dve.wait_ge(xsplit[m], ln_count(ph, which, k, 2) + 1)
                        nc.vector.tensor_tensor(lo, xt[:, m, :], hi.bitcast(F32), ALU.subtract)\
                            .then_inc(xsplit[m], 1)
                    if s[0] == "route":
                        which, k = s[1], s[2]
                        n = call(which, k)

                        def step(j):
                            dve.wait_ge(gate_step, ph.count(lambda o: GATE_STEPS * call(which, k + o) + j))

                        dve.wait_ge(shared_filled, shared_count(ph, s))
                        if n >= 1:
                            dve.wait_ge(gate_exp, ph.count(lambda o: call(which, k + o)))
                        nc.vector.tensor_tensor(logit[:, :, :],
                                                shared_ps[:, 0:TT * E].rearrange("p (t e) -> p t e", e=E),
                                                br_bc[:, :].unsqueeze(1).broadcast_to([P, TT, E]), ALU.add)\
                            .then_inc(shared_emptied, 1)
                        dve.wait_ge(shared_emptied, shared_count(ph, s))
                        nc.vector.tensor_reduce(out=top[:, :], in_=logit[:, :, :], op=ALU.max, axis=AX.X)\
                            .then_inc(gate_step, 1)
                        step(1)
                        nc.vector.tensor_tensor(below[:, :, :], logit[:, :, :],
                                                top[:, :].unsqueeze(2).broadcast_to([P, TT, E]), ALU.subtract)\
                            .then_inc(gate_step, 1)
                        other = logit[:, :, :].unsqueeze(2).broadcast_to([P, TT, E, E])
                        own = logit[:, :, :].unsqueeze(3).broadcast_to([P, TT, E, E])
                        nc.vector.tensor_tensor(beats[:, :, :, :], other, own, ALU.is_gt).then_inc(gate_step, 1)
                        nc.vector.tensor_tensor(ties[:, :, :, :], other, own, ALU.is_equal).then_inc(gate_step, 1)
                        step(4)
                        nc.vector.tensor_tensor(ties[:, :, :, :], ties[:, :, :, :],
                                                tri_sb[:, :, :].unsqueeze(1).broadcast_to([P, TT, E, E]), ALU.mult)\
                            .then_inc(gate_step, 1)
                        step(5)
                        nc.vector.tensor_tensor(beats[:, :, :, :], beats[:, :, :, :], ties[:, :, :, :], ALU.add)\
                            .then_inc(gate_step, 1)
                        step(6)
                        nc.vector.tensor_reduce(out=rank[:, :, :], in_=beats[:, :, :, :], op=ALU.add, axis=AX.X)\
                            .then_inc(gate_step, 1)
                        step(7)
                        dve.wait_ge(gate_exp, ph.count(lambda o: call(which, k + o) + 1))
                        nc.vector.scalar_tensor_tensor(out=chosen[:, :, :], in0=rank[:, :, :], scalar=1.5,
                                                       in1=expd[:, :, :], op0=ALU.is_lt, op1=ALU.mult)\
                            .then_inc(gate_step, 1)
                        step(8)
                        nc.vector.tensor_reduce(out=gsum[:, :], in_=chosen[:, :, :], op=ALU.add, axis=AX.X)\
                            .then_inc(gate_step, 1)
                        step(9)
                        nc.vector.reciprocal(grec[:, :], gsum[:, :]).then_inc(gate_step, 1)
                        step(10)
                        nc.vector.scalar_tensor_tensor(out=gates[:, n % 2, :, :], in0=chosen[:, :, :], scalar=0.5,
                                                       in1=grec[:, :].unsqueeze(2).broadcast_to([P, TT, E]),
                                                       op0=ALU.mult, op1=ALU.mult).then_inc(gates_done, 1)
                    if s[0] == "bias_down":
                        which, k = s[1], s[2]
                        res, acc = (x_in, x1) if which == 1 else (x2, y_out)
                        dve.wait_ge(shared_filled, shared_count(ph, s))
                        if which == 1 and k >= 2:
                            dve.wait_ge(x2_seeded, ph.count(lambda o: k + o - 1))
                        if which == 2 and k >= 2:
                            dve.wait_ge(out_stored[k % 2], ph.count(lambda o: 16 * ((k + o) // 2)))
                        nc.vector.tensor_tensor(acc[:, k % 2, :, :],
                                                shared_ps[:, :].rearrange("p (t d) -> p t d", d=D),
                                                res[:, k % 2, :, :], ALU.add).then_inc(shared_emptied, 1)
                    if s[0] == "project_q":
                        c = s[1]

                        def step(j):
                            dve.wait_ge(qsplit, ph.count(lambda o: SPLIT_STEPS * (c + o) + j))

                        dve.wait_ge(shared_emptied, shared_count(ph, s))
                        if c >= 1:
                            dve.wait_ge(qk_out, ph.count(lambda o: 96 * (c + o)))
                        nc.vector.tensor_copy(q_part[:, 0, :], q_f[:, :]).then_inc(qsplit, 1)
                        step(1)
                        nc.vector.tensor_tensor(q_rest[:, :], q_f[:, :], q_part[:, 0, :], ALU.subtract)\
                            .then_inc(qsplit, 1)
                        step(2)
                        nc.vector.tensor_copy(q_part[:, 1, :], q_rest[:, :]).then_inc(qsplit, 1)
                        step(3)
                        nc.vector.tensor_tensor(q_part[:, 2, :], q_rest[:, :], q_part[:, 1, :], ALU.subtract)\
                            .then_inc(qsplit, 1)
                    if s[0] == "project_v":
                        c = s[1]
                        dve.wait_ge(shared_filled, shared_count(ph, s))
                        if c == 0:
                            dve.wait_ge(cleared, 2)
                        if c >= 2:
                            dve.wait_ge(pv_filled, ph.count(lambda o: 4 * (c + o - 1)))
                        for tt in range(TT):
                            last = nc.vector.tensor_tensor(
                                v_st[c % 2][:, tt, :, 0:HD],
                                shared_ps[:, tt * D:(tt + 1) * D].rearrange("p (h d) -> p h d", d=HD),
                                bv_bc[:, :].rearrange("p (h d) -> p h d", d=HD), ALU.add)
                        last.then_inc(shared_emptied, 1)
                    if s[0] == "score_max":
                        c, h = s[1], s[2]
                        dve.wait_ge(max_filled, ph.count(lambda o: H * (c + o) + h + 1))
                        if c >= 1 and h == 0:
                            dve.wait_ge(max_step, ph.count(lambda o: MAX_STEPS * (c + o - 1) + 1))
                        nc.vector.tensor_reduce(out=mx[:, 1::2, h], in_=score_ps[:, :, P:3 * P], op=ALU.max, axis=AX.X)
                        nc.vector.tensor_reduce(out=mx[:, 0::2, h], in_=score_ps[:, :, 0:P], op=ALU.max, axis=AX.X)\
                            .then_inc(max_taken, 1)
                    if s[0] == "send_max":
                        c = s[1]

                        def step(j):
                            dve.wait_ge(max_step, ph.count(lambda o: MAX_STEPS * (c + o) + j))

                        dve.wait_ge(max_taken, ph.count(lambda o: H * (c + o) + H))
                        flat = neg_mx[:, :, :, :].rearrange("p t a h -> p t (a h)")
                        rest = mx_rest[:, :].rearrange("p (t h) -> p t h", h=H)
                        nc.vector.tensor_scalar(neg_mx[:, :, :, :],
                                                mx[:, :, :].rearrange("p t (h a) -> p t a h", a=2), -1.0, None,
                                                ALU.mult).then_inc(max_step, 1)
                        step(1)
                        if c >= 1:
                            dve.wait_ge(shared_filled, shared_count(ph, ("send_max", c - 1)))
                        nc.vector.tensor_copy(mx_part[:, :, 0, :], flat).then_inc(max_step, 1)
                        step(2)
                        nc.vector.tensor_tensor(rest, flat, mx_part[:, :, 0, :], ALU.subtract).then_inc(max_step, 1)
                        step(3)
                        nc.vector.tensor_copy(mx_part[:, :, 1, :], rest).then_inc(max_step, 1)
                        step(4)
                        nc.vector.tensor_tensor(mx_part[:, :, 2, :], rest, mx_part[:, :, 1, :], ALU.subtract)\
                            .then_inc(max_step, 1)
                    if s[0] == "normalise":
                        c, tt = s[1], s[2]
                        dve.wait_ge(shared_filled, shared_count(ph, s))
                        if tt == 0 and c >= 1:
                            dve.wait_ge(shared_filled, shared_count(ph, ("transpose_o", c - 1)))
                        o = shared_ps[:, :].rearrange("p (h w) -> p h w", w=32)
                        nc.vector.reciprocal(o_rec[:, :].unsqueeze(2), o[:, :, HD:HD + 1]).then_inc(rec_done, 1)
                        dve.wait_ge(rec_done, ph.count(lambda q: TT * (c + q) + tt + 1))
                        nc.vector.tensor_tensor(o_n[:, tt, :].rearrange("p (h d) -> p h d", d=HD), o[:, :, 0:HD],
                                                o_rec[:, :].unsqueeze(2).broadcast_to([P, H, HD]), ALU.mult)\
                            .then_inc(shared_emptied, 1)
                    if s[0] == "project_o":
                        c = s[1]
                        dve.wait_ge(shared_filled, shared_count(ph, s))
                        dve.wait_ge(x2_seeded, ph.count(lambda o: c + o + 1))
                        nc.vector.tensor_tensor(x2[:, c % 2, :, :], shared_ps[:, :].rearrange("p (t d) -> p t d", d=D),
                                                x2[:, c % 2, :, :], ALU.add).then_inc(shared_emptied, 1)

            phases(dve, body)

        @block.tensor
        def _(pe):
            pe.wait_ge(loaded, 16 * LOADS)
            pe.wait_ge(weights_split, 5)
            mm, tr = nc.tensor.matmul, nc.tensor.transpose

            def three(out, hi, lo, x_hi, x_lo):
                mm(out, hi, x_hi, start=True, stop=False)
                mm(out, hi, x_lo, start=False, stop=False)
                return mm(out, lo, x_hi, start=False, stop=True)

            def body(ph):
                for s in steps(ph.c):
                    if s[0] in SHARED and SHARED_AT[s] > 0:
                        pe.wait_ge(shared_emptied, shared_count(ph, s) - 1)
                    if s[0] == "up":
                        which, k, t = s[1:]
                        n = call(which, k)
                        tile = ph.count(lambda o: HSLOT * call(which, k + o) + t)
                        if t == 0:
                            pe.wait_ge(xsplit[1], ph.count(lambda o: 2 * call(which, k + o) + 2))
                        if HSLOT * n + t >= 2:
                            pe.wait_ge(up_relued, tile - 1)
                        w = slice(t * P, (t + 1) * P)
                        three(up_ps[:, t % 2, :], w1_hi[:, w], w1_lo[:, w], xf_hi[:, n % 2, :], xf_lo[:, n % 2, :])\
                            .then_inc(up_filled, 1)
                    if s[0] == "down":
                        which, k, t = s[1:]
                        e, half = t // 2, t % 2
                        at = ph.count(lambda o: HSLOT * call(which, k + o) + t)
                        if half == 0:
                            pe.wait_ge(up_relued, at + 2)
                        if HSLOT * call(which, k) + t >= 2:
                            pe.wait_ge(down_added, at - 1)
                        for tt in (2 * half, 2 * half + 1):
                            for j in range(2):
                                last = mm(down_ps[:, half, tt % 2, :], hid[:, (2 * e + j) % 4, tt * P:(tt + 1) * P],
                                          w2_sb[:, e, j, :], start=j == 0, stop=j == 1)
                        last.then_inc(down_filled, 1)
                    if s[0] == "transpose_x":
                        which, k = s[1], s[2]
                        m = min(which, 1)
                        pe.wait_ge(xn_done[m], ln_count(ph, which, k, TT) + TT)
                        for tt in range(TT):
                            last = tr(shared_ps[:, tt * P:(tt + 1) * P], xn[:, m, tt, :], id_f[:, :])
                        last.then_inc(shared_filled, 1)
                    if s[0] == "route":
                        pe.wait_ge(shared_emptied, shared_count(ph, ("transpose_x", s[1], s[2])))
                        for tt in range(TT):
                            last = mm(shared_ps[:, tt * E:(tt + 1) * E], xt[:, 1, tt * P:(tt + 1) * P], wr_sb[:, :],
                                      start=True, stop=True)
                        last.then_inc(shared_filled, 1)
                    if s[0] == "transpose_g":
                        which, k = s[1], s[2]
                        n = call(which, k)
                        pe.wait_ge(gates_done, ph.count(lambda o: call(which, k + o) + 1))
                        hold(pe)
                        for tt in range(TT):
                            last = tr(shared_ps[0:E, tt * P:(tt + 1) * P], gates[:, n % 2, tt, :], id_f[:, :])
                        last.then_inc(shared_filled, 1)
                    if s[0] == "bias_down":
                        for tt in range(TT):
                            last = mm(shared_ps[:, tt * D:(tt + 1) * D], gates_t[:, tt * P:(tt + 1) * P], b2_sb[:, :],
                                      start=True, stop=True)
                        last.then_inc(shared_filled, 1)
                    if s[0] in ("project_q", "project_k"):
                        c, j = s[1], int(s[0] == "project_k")
                        pe.wait_ge(xsplit[0], ph.count(lambda o: 2 * (c + o) + 2))
                        three(shared_ps[:, :], wqk_hi[:, j, :], wqk_lo[:, j, :], xa_hi[:, :], xa_lo[:, :])\
                            .then_inc(shared_filled, 1)
                    if s[0] == "project_v":
                        for tt in range(TT):
                            last = mm(shared_ps[:, tt * D:(tt + 1) * D], xt[:, 0, tt * P:(tt + 1) * P], wv_sb[:, :],
                                      start=True, stop=True)
                        last.then_inc(shared_filled, 1)
                    if s[0] == "score_max":
                        c, h = s[1], s[2]
                        if h == 0:
                            pe.wait_ge(qk_in, ph.count(lambda o: 64 * (c + o + 1)))
                            if c >= 1:
                                pe.wait_ge(exp_done, ph.count(lambda o: H * (c + o)))
                        else:
                            pe.wait_ge(max_taken, ph.count(lambda o: H * (c + o) + h))
                        rows = slice(64 * (h % 2), 64 * (h % 2) + ROWS_A)
                        q, k = q_st[c % 2], k_st[c % 2]
                        for b in range(2):
                            i0 = b * T
                            for i, cols in ((0, slice(0, P)), (1, slice(P, 3 * P))):
                                mm(score_ps[:, b, cols], q[rows, h // 2, i0 + i * P:i0 + (i + 1) * P],
                                   k[rows, h // 2, i0:i0 + (i + 1) * P], start=True, stop=False)
                                last = mm(score_ps[:, b, cols.stop - P:cols.stop], id_b[:, :], mask_sb[:, :],
                                          start=False, stop=True)
                        last.then_inc(max_filled, 1)
                    if s[0] == "send_max":
                        c = s[1]
                        pe.wait_ge(max_step, ph.count(lambda o: MAX_STEPS * (c + o + 1)))
                        hold(pe)
                        for tt in range(TT):
                            last = tr(shared_bf[0:3 * H, tt * P:(tt + 1) * P], mx_part[:, tt, :, :], id_b[:, :])
                        last.then_inc(shared_filled, 1)
                    if s[0] == "score_exp":
                        c, h = s[1], s[2]
                        if h == 0:
                            pe.wait_ge(max_in, ph.count(lambda o: 96 * (c + o + 1)))
                            pe.wait_ge(max_taken, ph.count(lambda o: H * (c + o) + H))
                        else:
                            pe.wait_ge(exp_done, ph.count(lambda o: H * (c + o) + h))
                        rows = slice(64 * (h % 2), 64 * (h % 2) + ROWS_B)
                        q, k = q_st[c % 2], k_st[c % 2]
                        for b in range(2):
                            for j, cols in ((0, slice(0, 2 * P)), (1, slice(2 * P, 3 * P))):
                                mm(score_ps[:, b, cols], k[rows, h // 2, b * T + j * P:b * T + (j + 1) * P],
                                   q[rows, h // 2, b * T + j * P:(b + 1) * T], start=True, stop=False)
                                last = mm(score_ps[:, b, cols.start:cols.start + P], mask_sb[:, :], id_b[:, :],
                                          start=False, stop=True)
                        last.then_inc(exp_filled, 1)
                    if s[0] == "pv":
                        c, g = s[1], s[2]
                        pe.wait_ge(exp_done, ph.count(lambda o: H * (c + o) + 4 * g + 4))
                        if 4 * c + g >= 1:
                            pe.wait_ge(o_copied, ph.count(lambda o: 4 * (c + o) + g))
                        for b in range(2):
                            for j in range(2):
                                for hh in range(4):
                                    h = 4 * g + hh
                                    p = prob[:, h % 8, b, 0:2, :] if j == 0 else prob[:, h % 8, b, 2:3, :]
                                    last = mm(o_ps[32 * hh:32 * hh + 32, b * T + j * P:(b + 1) * T],
                                              v_st[c % 2][:, 2 * b + j, h, :], p, start=j == 0, stop=j == 1)
                        last.then_inc(pv_filled, 1)
                    if s[0] == "normalise":
                        c, tt = s[1], s[2]
                        if tt == 0:
                            pe.wait_ge(o_copied, ph.count(lambda o: 4 * (c + o) + 4))
                        for g in range(4):
                            last = tr(shared_ps[:, g * P:(g + 1) * P], o_t[:, g, tt * P:(tt + 1) * P], id_f[:, :])
                        last.then_inc(shared_filled, 1)
                    if s[0] == "transpose_o":
                        for tt in range(TT):
                            last = tr(shared_ps[:, tt * P:(tt + 1) * P], o_n[:, tt, :], id_f[:, :])
                        last.then_inc(shared_filled, 1)
                    if s[0] == "project_o":
                        for tt in range(TT):
                            last = mm(shared_ps[:, tt * D:(tt + 1) * D], o_nt[:, tt * P:(tt + 1) * P], wo_sb[:, :],
                                      start=True, stop=True)
                        last.then_inc(shared_filled, 1)

            phases(pe, body)


def kernel(L0_attn_x, L0_attn_Wq, L0_attn_bq, L0_attn_Wk, L0_attn_bk, L0_attn_Wv, L0_attn_bv, L0_attn_Wo,
           L0_attn_bo, L0_ffn_Wr, L0_ffn_br, L0_ffn_W1, L0_ffn_b1, L0_ffn_W2, L0_ffn_b2):
    import numpy as np
    import ml_dtypes
    import concourse.bacc as bacc
    from concourse.bass_utils import run_bass_kernel_spmd

    lay = np.ascontiguousarray
    a = {
        "x": lay(np.asarray(L0_attn_x).reshape(B * T, D)),
        "wq": lay(np.asarray(L0_attn_Wq).T), "bq": lay(np.asarray(L0_attn_bq).reshape(D, 1)),
        "wk": lay(np.asarray(L0_attn_Wk).T), "bk": lay(np.asarray(L0_attn_bk).reshape(D, 1)),
        "wv": lay(np.asarray(L0_attn_Wv).T), "bv": lay(np.asarray(L0_attn_bv)),
        "wo": lay(np.asarray(L0_attn_Wo).T), "bo": lay(np.asarray(L0_attn_bo)),
        "wr": lay(np.asarray(L0_ffn_Wr)), "br": lay(np.asarray(L0_ffn_br)),
        "w1": lay(np.asarray(L0_ffn_W1).transpose(1, 0, 2).reshape(D, E * HID)),
        "b1": lay(np.asarray(L0_ffn_b1).reshape(E * 2, P).T),
        "w2": lay(np.asarray(L0_ffn_W2).reshape(E, 2, P, D).transpose(2, 0, 1, 3)),
        "b2": lay(np.asarray(L0_ffn_b2)),
    }
    bf = ml_dtypes.bfloat16
    a["ident"] = np.eye(P, dtype=np.float32)
    a["ident_b"] = np.eye(P, dtype=bf)
    a["mask_b"] = np.triu(np.full((P, P), -1e30, np.float32), 1).astype(bf)
    a["tri"] = np.tril(np.ones((E, E), np.float32), -1).reshape(E * E)
    pos = np.tile(np.arange(T, dtype=np.float32), 2)
    rows_q = np.zeros((64 - ROWS_QK, H // 2, CH), np.float32)
    rows_k = np.zeros((64 - ROWS_QK, H // 2, CH), np.float32)
    rows_q[0], rows_q[1] = 1.0, -pos
    rows_k[0], rows_k[1:5] = pos, 1.0
    a["qrows"], a["krows"] = rows_q.astype(bf), rows_k.astype(bf)

    nc = bacc.Bacc("TRN2", target_bir_lowering=False, num_devices=1)
    arrays, args = {}, []
    for name, arr in a.items():
        arrays[name + "_dram"] = arr
        args.append(nc.dram_tensor(name + "_dram", arr.shape, mybir.dt.from_np(arr.dtype), kind="ExternalInput").ap())
    for name in ("zq", "zk"):
        args.append(nc.dram_tensor(name, [2, P, PIECES, CH], BF16, kind="Internal").ap())
    args.append(nc.dram_tensor("out_dram", [B * T, D], F32, kind="ExternalOutput").ap())
    macaron_kernel(nc, *args)
    r = run_bass_kernel_spmd(nc, [arrays], core_ids=[0])
    return r.results[0]["out_dram"].reshape(B, T, D)
```

```python
import concourse.bass as bass
from concourse import mybir
from contextlib import ExitStack

F32 = mybir.dt.float32
F32R = mybir.dt.float32r
BF16 = mybir.dt.bfloat16
ALU = mybir.AluOpType
ACT = mybir.ActivationFunctionType
AX = mybir.AxisListType

P = 128
D = 128
T = 256
B = 32
CH = 512
TT = CH // P
NC = B * T // CH
H, HD = 16, 8
E, HID = 8, 256
EPS = 1e-5
QSCALE = 1.0 / float(HD) ** 0.5
PIECES = 6
ROWS_QK = PIECES * HD
ROWS_A = ROWS_QK + 2
ROWS_M = ROWS_A + 3
MASKED = ((0, 128), (0, 64), (64, 64))
ROWS_B = ROWS_M + 2 * len(MASKED)
HSLOT = 16

LOOP_FROM, LOOP_TO = 2, 14


def call_ff1(k):
    return k if k < 2 else 2 * k - 2


def call_ff2(k):
    return 2 * k + 3 if k < NC - 2 else 16 + k


def steps(c):
    def there(k):
        return 0 <= k < NC

    places = [(k, place) for k in range(16, 32) for place in range(3)]
    exp_at = [places[u * len(places) // (2 * H)] for u in range(2 * H)]
    out = []
    if there(c + 2) and c + 2 >= 2:
        out.append(("load_x", c + 2))
    for k in range(32):
        if k < HSLOT and there(c + 1):
            out.append(("up", 1, c + 1, k))
        if k >= HSLOT and there(c - 1):
            out.append(("up", 2, c - 1, k - HSLOT))
        def score(place):
            if there(c) and k < H and place != 1:
                out.append(("score_max", c, k, place // 2))
            if there(c) and (k, place) in exp_at:
                u = exp_at.index((k, place))
                out.append(("score_exp", c, u // 2, u % 2))
                if u % 8 == 4 and u > 8:
                    out.append(("pv", c, u // 8 - 1))

        down = None
        if k < 2 and there(c - 2):
            down = ("down", 2, c - 2, 14 + k)
        if 2 <= k < 18 and there(c + 1):
            down = ("down", 1, c + 1, k - 2)
        if k >= 18 and there(c - 1):
            down = ("down", 2, c - 1, k - 18)
        score(0)
        if down:
            out.append(down + (0,))
        score(1)
        if down:
            out.append(down + (1,))
        score(2)
        if k == 2 and there(c - 2):
            out.append(("store", c - 2))
        if there(c - 1):
            if k == 1:
                out.append(("pv", c - 1, 3))
                out.append(("seed_x2", c - 1))
            if 3 <= k <= 6:
                out.append(("normalise", c - 1, k - 3))
            if k == 7:
                out.append(("transpose_o", c - 1))
            if k == 8:
                out.append(("project_o", c - 1))
                out.append(("ln_stats", 2, c - 1))
            if k == 9:
                out.append(("ln_apply", 2, c - 1))
            if k == 10:
                out.append(("transpose_x", 2, c - 1))
            if k == 11:
                out.append(("route", 2, c - 1))
            if k == 12:
                out.append(("gate", 2, c - 1))
            if k == 13:
                out.append(("gate_end", 2, c - 1))
            if k == 14:
                out.append(("transpose_g", 2, c - 1))
            if k == 15:
                out.append(("bias_down", 2, c - 1))
        if there(c) and k in (8, 16):
            out.append(("split_max", c, k // 16))
        if there(c) and k in (9, 17):
            out.append(("send_max", c, k // 16))
        if there(c + 1):
            if k == 18:
                out.append(("ln_stats", 0, c + 1))
            if k == 19:
                out.append(("ln_apply", 0, c + 1))
            if k == 20:
                out.append(("transpose_x", 0, c + 1))
            if k == 21:
                out.append(("project_q", c + 1))
            if k == 22:
                out.append(("project_k", c + 1))
            if k == 23:
                out.append(("project_v", c + 1))
        if there(c + 2):
            if k == 24:
                out.append(("ln_stats", 1, c + 2))
            if k == 25:
                out.append(("ln_apply", 1, c + 2))
            if k == 26:
                out.append(("transpose_x", 1, c + 2))
            if k == 27:
                out.append(("route", 1, c + 2))
            if k == 28:
                out.append(("gate", 1, c + 2))
            if k == 29:
                out.append(("gate_end", 1, c + 2))
            if k == 30:
                out.append(("transpose_g", 1, c + 2))
            if k == 31:
                out.append(("bias_down", 1, c + 2))
    return out


SHARED = ("normalise", "transpose_o", "project_o", "transpose_x", "route", "gate", "transpose_g",
          "bias_down", "send_max", "project_q", "project_k", "project_v")
SHARED_AT = {s: n for n, s in enumerate(s for c in range(-2, NC + 2) for s in steps(c) if s[0] in SHARED)}


def macaron_kernel(nc, x, wq, bq, wk, bk, wv, bv, wo, bo, wr, br, w1, b1, w2, b2,
                   ident, ident_b, mask, tri, qrows, krows, zq, zk, out):
    x_v = x.rearrange("(c t p) d -> c p t d", t=TT, p=P)
    out_v = out.rearrange("(c t p) d -> c p t d", t=TT, p=P)

    with ExitStack() as ctx:
        def sb(name, shape, dt=F32):
            return ctx.enter_context(nc.sbuf_tensor(name, shape, dt))

        def sem(name):
            return ctx.enter_context(nc.semaphore(name))

        w1_f = sb("w1_f", [P, E * HID])
        w1_hi = sb("w1_hi", [P, E * HID], F32R)
        w1_lo = sb("w1_lo", [P, E * HID], F32R)
        w2_sb = sb("w2_sb", [P, E, 2, D])
        b1_sb = sb("b1_sb", [P, E * 2])
        b2_sb = sb("b2_sb", [E, D])
        wr_f = sb("wr_f", [P, E])
        wr_hi = sb("wr_hi", [P, P], F32R)
        wr_lo = sb("wr_lo", [P, P], F32R)
        br_sb = sb("br_sb", [E, 1])
        logit_t = sb("logit_t", [E, CH])
        wqk_f = sb("wqk_f", [P, 2, D])
        wqk_hi = sb("wqk_hi", [P, 2, D], F32R)
        wqk_lo = sb("wqk_lo", [P, 2, D], F32R)
        wv_sb = sb("wv_sb", [P, D])
        wo_sb = sb("wo_sb", [P, D])
        bq_sb = sb("bq_sb", [P, 1])
        bqs_sb = sb("bqs_sb", [P, 1])
        bk_sb = sb("bk_sb", [P, 1])
        bv_bc = sb("bv_bc", [P, D])
        bo_bc = sb("bo_bc", [P, D])
        id_f = sb("id_f", [P, P])
        id_b = sb("id_b", [P, P], BF16)
        mask_sb = sb("mask_sb", [P, 2 * P])
        score_junk = sb("score_junk", [P, 2, 3 * P], BF16)
        tri_sb = sb("tri_sb", [P, E, E])
        minus_half = sb("minus_half", [P, TT])
        x_in = sb("x_in", [P, 2, TT, D])
        x1 = sb("x1", [P, 2, TT, D])
        x2 = sb("x2", [P, 2, TT, D])
        y_out = sb("y_out", [P, 2, TT, D])
        stats = sb("stats", [P, 2, TT, 6])
        mv = sb("mv", [P, 2, TT, 2])
        var_eps = sb("var_eps", [P, 2, TT])
        rstd = sb("rstd", [P, 2, TT])
        xn = sb("xn", [P, 2, TT, D])
        xt = sb("xt", [P, CH])
        xa_hi = sb("xa_hi", [P, CH], F32R)
        xa_lo = sb("xa_lo", [P, CH], F32R)
        xf_hi = sb("xf_hi", [P, 2, CH], F32R)
        xf_lo = sb("xf_lo", [P, 2, CH], F32R)
        logit = sb("logit", [P, TT, E])
        top = sb("top", [P, TT])
        below = sb("below", [P, TT, E])
        expd = sb("expd", [P, TT, E])
        beats = sb("beats", [P, TT, E, E])
        ties = sb("ties", [P, TT, E, E])
        rank = sb("rank", [P, TT, E])
        chosen = sb("chosen", [P, TT, E])
        gsum = sb("gsum", [P, TT])
        grec = sb("grec", [P, TT])
        gates = sb("gates", [P, 2, TT, E])
        gates_t = sb("gates_t", [E, CH])
        hid = sb("hid", [P, 4, CH])
        q_f = sb("q_f", [P, CH])
        k_f = sb("k_f", [P, CH])
        q_rest = sb("q_rest", [P, CH])
        k_rest = sb("k_rest", [P, CH])
        q_part = sb("q_part", [P, 3, CH], BF16)
        k_part = sb("k_part", [P, 3, CH], BF16)
        q_st = [sb(f"q_st{i}", [P, H // 2, CH], BF16) for i in range(2)]
        k_st = [sb(f"k_st{i}", [P, H // 2, CH], BF16) for i in range(2)]
        v_st = [sb(f"v_st{i}", [P, TT, H, 32]) for i in range(2)]
        mx = sb("mx", [P, TT, H])
        neg_mx = sb("neg_mx", [P, TT, 2, 2, H // 4])
        mx_rest = sb("mx_rest", [P, 2, TT, H // 2])
        mx_part = sb("mx_part", [P, TT, 2, 3, H // 2], BF16)
        mx_t = sb("mx_t", [3 * H // 2, 2, CH], BF16)
        prob = sb("prob", [P, 8, 2, 3, P])
        o_t = sb("o_t", [P, 4, CH])
        o_rec = sb("o_rec", [P, H])
        o_n = sb("o_n", [P, TT, D])
        o_nt = sb("o_nt", [P, CH])

        up_ps = ctx.enter_context(nc.psum_tensor("up_ps", [P, 2, CH], F32))
        down_ps = ctx.enter_context(nc.psum_tensor("down_ps", [P, 2, TT, D], F32))
        score_ps = ctx.enter_context(nc.psum_tensor("score_ps", [P, 2, CH], F32))
        o_ps = ctx.enter_context(nc.psum_tensor("o_ps", [P, CH], F32))
        shared_ps = ctx.enter_context(nc.psum_tensor("shared_ps", [P, CH], F32))
        shared_bf = shared_ps[:, :].bitcast(BF16)

        loaded = sem("loaded")
        weights_split = sem("weights_split")
        rows_cleared = sem("rows_cleared")
        cleared = sem("cleared")
        x_loaded = [sem(f"x_loaded{i}") for i in range(2)]
        out_stored = [sem(f"out_stored{i}") for i in range(2)]
        up_filled = sem("up_filled")
        up_relued = sem("up_relued")
        down_filled = sem("down_filled")
        down_added = sem("down_added")
        stats_done = [sem(f"stats_done{i}") for i in range(2)]
        moments_done = [sem(f"moments_done{i}") for i in range(2)]
        var_done = [sem(f"var_done{i}") for i in range(2)]
        rstd_done = [sem(f"rstd_done{i}") for i in range(2)]
        xn_done = [sem(f"xn_done{i}") for i in range(2)]
        xsplit = sem("xsplit")
        xf_hi_done = sem("xf_hi_done")
        shared_filled = sem("shared_filled")
        shared_emptied = sem("shared_emptied")
        gate_step = sem("gate_step")
        gates_done = sem("gates_done")
        gate_exp = sem("gate_exp")
        qsplit = sem("qsplit")
        ksplit = sem("ksplit")
        qk_out = sem("qk_out")
        qk_in = sem("qk_in")
        max_filled = sem("max_filled")
        max_taken = sem("max_taken")
        max_step = sem("max_step")
        max_in = [sem(f"max_in{g}") for g in range(2)]
        exp_filled = sem("exp_filled")
        exp_done = sem("exp_done")
        causal_done = sem("causal_done")
        pv_filled = sem("pv_filled")
        o_copied = sem("o_copied")
        rec_done = sem("rec_done")
        held = sem("held")
        x2_seeded = sem("x2_seeded")

        LOADS = 26
        GATE_STEPS, SPLIT_STEPS, MAX_STEPS = 10, 4, 10

        block = ctx.enter_context(nc.Block())

        class Phase:

            def __init__(self, c, i=None):
                self.c, self.i = c, i

            def count(self, f):
                if self.i is None:
                    return f(0)
                return f(0) + self.i * (f(2) - f(0))

        def phases(eng, body):
            for c in range(-2, LOOP_FROM):
                body(Phase(c))
            with eng.Fori(0, (LOOP_TO - LOOP_FROM) // 2) as i:
                for c in range(LOOP_FROM, LOOP_FROM + 2):
                    body(Phase(c, i))
            for c in range(LOOP_TO, NC + 2):
                body(Phase(c))

        def shared_count(ph, s):
            def f(o):
                at = s[:-1] + (s[-1] + o,) if s[0] in ("transpose_x", "route", "gate", "transpose_g", "bias_down", "transpose_o",
                                                       "project_o", "project_q", "project_k",
                                                       "project_v") else (s[0], s[1] + o, s[2])
                return SHARED_AT[at] + 1
            return ph.count(f)

        def call(which, k):
            return call_ff1(k) if which == 1 else call_ff2(k)

        def hold(eng):
            eng.sem_inc(held, 1)

        def ln_count(ph, which, k, per):
            return ph.count(lambda o: per * (k + o if which == 0 else call(which, k + o)))

        @block.sync
        def _(sp):
            for dst, src in ((w1_f[:, :], w1), (w2_sb[:, :, :, :], w2), (b1_sb[:, :], b1), (b2_sb[:, :], b2),
                             (wr_f[:, :], wr), (br_sb[:, :], br),
                             (wqk_f[:, 0, :], wq), (wqk_f[:, 1, :], wk), (wv_sb[:, :], wv), (wo_sb[:, :], wo),
                             (bq_sb[:, :], bq), (bk_sb[:, :], bk), (bv_bc[:, :], bv.partition_broadcast(P)),
                             (bo_bc[:, :], bo.partition_broadcast(P)), (id_f[:, :], ident), (id_b[:, :], ident_b),
                             (mask_sb[:, :], mask), (tri_sb[:, :, :].rearrange("p e f -> p (e f)"),
                                                       tri.partition_broadcast(P))):
                sp.dma_start(dst, src).then_inc(loaded, 16)
            for st, rows in ((q_st, qrows), (k_st, krows)):
                sp.dma_start(st[0][ROWS_QK:64, :, :], rows).then_inc(loaded, 16)
            for st, rows in ((q_st, qrows), (k_st, krows)):
                for i, a in ((0, 1), (1, 0), (1, 1)):
                    sp.dma_start(st[i][64 * a + ROWS_QK:64 * a + 64, :, :], rows).then_inc(loaded, 16)
            for k in range(2):
                sp.dma_start(x_in[:, k, :, :], x_v[k]).then_inc(x_loaded[k], 16)

            def body(ph):
                for s in steps(ph.c):
                    if s[0] == "load_x":
                        k = s[1]
                        sp.wait_ge(shared_emptied, shared_count(ph, ("bias_down", 1, k - 2)))
                        hold(sp)
                        sp.dma_start(x_in[:, k % 2, :, :], x_v[ph.count(lambda o: k + o)])\
                            .then_inc(x_loaded[k % 2], 16)
                    if s[0] == "store":
                        k = s[1]
                        sp.wait_ge(down_added, ph.count(lambda o: 16 * call_ff2(k + o) + 16))
                        hold(sp)
                        sp.dma_start(out_v[ph.count(lambda o: k + o)], y_out[:, k % 2, :, :])\
                            .then_inc(out_stored[k % 2], 16)
                    if s[0] == "send_max":
                        c, g = s[1:]
                        sp.wait_ge(shared_emptied, shared_count(ph, s))
                        hold(sp)
                        n = H // 4
                        for a in range(2):
                            for piece in range(3):
                                row = 64 * a + ROWS_A + piece
                                src = (2 * piece + a) * n
                                sp.dma_start(q_st[c % 2][row:row + 1, g * n:(g + 1) * n, :], mx_t[src:src + n, g, :])\
                                    .then_inc(max_in[g], 16)
                    if s[0] == "project_v":
                        c = s[1]
                        sp.wait_ge(qsplit, ph.count(lambda o: SPLIT_STEPS * (c + o + 1)))
                        hold(sp)
                        for z, part, dup in ((zq, q_part, False), (zk, k_part, True)):
                            if dup:
                                sp.wait_ge(ksplit, ph.count(lambda o: SPLIT_STEPS * (c + o + 1)))
                                hold(sp)
                                src = (part[:, 0:1, :].broadcast_to([P, 3, CH]),
                                       part[:, 1:2, :].broadcast_to([P, 2, CH]), part[:, 2:3, :])
                            else:
                                src = (part[:, 0:3, :], part[:, 0:2, :], part[:, 0:1, :])
                            for (r0, r1), sr in zip(((0, 3), (3, 5), (5, 6)), src):
                                sp.dma_start(z[c % 2, :, r0:r1, :], sr).then_inc(qk_out, 16)
                        sp.wait_ge(qk_out, ph.count(lambda o: 96 * (c + o + 1)))
                        hold(sp)
                        if c >= 2:
                            sp.wait_ge(exp_filled, ph.count(lambda o: 2 * H * (c + o - 1)))
                            hold(sp)
                        for z, st in ((zq, q_st), (zk, k_st)):
                            zr = z[c % 2].rearrange("(t a d) r n -> a (d r) t n", a=2, d=HD)
                            for a in range(2):
                                sp.dma_start(st[c % 2][64 * a:64 * a + ROWS_QK, :, :], zr[a]).then_inc(qk_in, 16)

            phases(sp, body)
            for k in range(2):
                sp.wait_ge(out_stored[k], 16 * NC // 2)

        @block.gpsimd
        def _(pool):
            for st in v_st:
                nc.gpsimd.memset(st[:, :, :, :], 0.0)
            nc.gpsimd.memset(minus_half[:, :], -0.5).then_inc(cleared, 1)
            pool.wait_ge(cleared, 1)
            for st in v_st:
                last = nc.gpsimd.memset(st[:, :, :, HD:HD + 1], 1.0)
            last.then_inc(cleared, 1)
            pool.wait_ge(loaded, 16 * LOADS)

            def body(ph):
                for s in steps(ph.c):
                    if s[0] == "ln_stats":
                        which, k = s[1], s[2]
                        m = min(which, 1)
                        pool.wait_ge(moments_done[m], ln_count(ph, which, k, TT) + TT)
                        hold(pool)
                        nc.gpsimd.tensor_scalar(var_eps[:, m, :], mv[:, m, :, 1], EPS, None, ALU.add)\
                            .then_inc(var_done[m], 1)
                        pool.wait_ge(var_done[m], ln_count(ph, which, k, 1) + 1)
                        nc.gpsimd.tensor_tensor(rstd[:, m, :], var_eps[:, m, :], minus_half[:, :], ALU.pow)\
                            .then_inc(rstd_done[m], 1)
                    if s[0] == "seed_x2":
                        c = s[1]
                        pool.wait_ge(down_added, ph.count(lambda o: 16 * call_ff1(c + o) + 16))
                        if c >= 2:
                            pool.wait_ge(shared_emptied, shared_count(ph, ("bias_down", 2, c - 2)))
                        nc.gpsimd.tensor_tensor(x2[:, c % 2, :, :], x1[:, c % 2, :, :],
                                                bo_bc[:, :].unsqueeze(1).broadcast_to([P, TT, D]), ALU.add)\
                            .then_inc(x2_seeded, 1)
                    if s[0] == "project_k":
                        c = s[1]

                        def step(n):
                            return ph.count(lambda o: SPLIT_STEPS * (c + o) + n)

                        pool.wait_ge(shared_emptied, shared_count(ph, s))
                        if c >= 1:
                            pool.wait_ge(qk_out, ph.count(lambda o: 96 * (c + o)))
                        hold(pool)
                        nc.gpsimd.tensor_copy(k_part[:, 0, :], k_f[:, :]).then_inc(ksplit, 1)
                        pool.wait_ge(ksplit, step(1))
                        nc.gpsimd.tensor_tensor(k_rest[:, :], k_f[:, :], k_part[:, 0, :], ALU.subtract)\
                            .then_inc(ksplit, 1)
                        pool.wait_ge(ksplit, step(2))
                        hold(pool)
                        nc.gpsimd.tensor_copy(k_part[:, 1, :], k_rest[:, :]).then_inc(ksplit, 1)
                        pool.wait_ge(ksplit, step(3))
                        nc.gpsimd.tensor_tensor(k_part[:, 2, :], k_rest[:, :], k_part[:, 1, :], ALU.subtract)\
                            .then_inc(ksplit, 1)

                    if s[0] == "score_exp":
                        c, h, b = s[1:]
                        pool.wait_ge(exp_done, ph.count(lambda o: 2 * H * (c + o) + 2 * h + b + 1))
                        hold(pool)
                        diag = prob[:, h % 8, b, 0:3:2, :]
                        nc.gpsimd.affine_select(out=diag, in_=diag, compare_op=ALU.is_ge, fill=0.0, base=0,
                                                pattern=[[0, 2], [1, P]], channel_multiplier=-1)\
                            .then_inc(causal_done, 1)

            phases(pool, body)

        @block.scalar
        def _(act):
            act.wait_ge(loaded, 16 * LOADS)
            act.wait_ge(weights_split, 7)

            def body(ph):
                for s in steps(ph.c):
                    if s[0] == "up":
                        which, k, t = s[1:]
                        tile = ph.count(lambda o: HSLOT * call(which, k + o) + t)
                        act.wait_ge(up_filled, tile + 1)
                        if HSLOT * call(which, k) + t >= 4:
                            act.wait_ge(down_filled, tile - t % 2 - 2)
                        nc.scalar.activation(hid[:, t % 4, :], up_ps[:, t % 2, :], ACT.Relu,
                                             bias=b1_sb[:, t:t + 1]).then_inc(up_relued, 1)
                    if s[0] == "score_exp":
                        c, h, b = s[1:]
                        act.wait_ge(exp_filled, ph.count(lambda o: 2 * H * (c + o) + 2 * h + b + 1))
                        if h % 4 == 0 and b == 0 and 4 * c + h // 4 >= 2:
                            act.wait_ge(pv_filled, ph.count(lambda o: 4 * (c + o) + h // 4 - 1))
                        nc.scalar.activation(prob[:, h % 8, b, :, :].rearrange("p s n -> p (s n)"),
                                             score_ps[:, b, 0:3 * P], ACT.Exp).then_inc(exp_done, 1)
                    if s[0] == "pv":
                        c, g = s[1], s[2]
                        act.wait_ge(pv_filled, ph.count(lambda o: 4 * (c + o) + g + 1))
                        if c >= 1 and g == 0:
                            act.wait_ge(shared_filled, shared_count(ph, ("normalise", c - 1, 3)))
                        nc.scalar.activation(o_t[:, g, :], o_ps[:, :], ACT.Copy).then_inc(o_copied, 1)
                    if s[0] == "transpose_x" and s[1] == 0:
                        k = s[2]
                        act.wait_ge(shared_filled, shared_count(ph, s))
                        if k >= 1:
                            act.wait_ge(xsplit, ph.count(lambda o: 2 * (k + o)))
                        nc.scalar.activation(xt[:, :], shared_ps[:, :], ACT.Copy).then_inc(shared_emptied, 1)
                    if s[0] == "transpose_x" and s[1] > 0:
                        which, k = s[1], s[2]
                        n = call(which, k)
                        act.wait_ge(shared_filled, shared_count(ph, s))
                        if n >= 2:
                            act.wait_ge(up_filled, ph.count(lambda o: HSLOT * (call(which, k + o) - 1)))
                        nc.scalar.activation(xf_hi[:, n % 2, :], shared_ps[:, :], ACT.Copy).then_inc(xf_hi_done, 1)
                    if s[0] == "route":
                        act.wait_ge(shared_filled, shared_count(ph, s))
                        nc.scalar.activation(logit_t[:, :], shared_ps[0:E, :], ACT.Identity, bias=br_sb[:, 0:1])\
                            .then_inc(shared_emptied, 1)
                    if s[0] == "gate":
                        which, k = s[1], s[2]
                        act.wait_ge(gate_step, ph.count(lambda o: GATE_STEPS * call(which, k + o) + 2))
                        nc.scalar.activation(expd[:, :, :], below[:, :, :], ACT.Exp).then_inc(gate_exp, 1)
                    if s[0] == "transpose_g":
                        act.wait_ge(shared_filled, shared_count(ph, s))
                        nc.scalar.activation(gates_t[:, :], shared_ps[0:E, :], ACT.Copy).then_inc(shared_emptied, 1)
                    if s[0] == "project_q":
                        c = s[1]
                        act.wait_ge(shared_filled, shared_count(ph, s))
                        if c >= 1:
                            act.wait_ge(qsplit, ph.count(lambda o: SPLIT_STEPS * (c + o)))
                        nc.scalar.activation(q_f[:, :], shared_ps[:, :], ACT.Identity, bias=bqs_sb[:, 0:1],
                                             scale=QSCALE).then_inc(shared_emptied, 1)
                    if s[0] == "project_k":
                        c = s[1]
                        act.wait_ge(shared_filled, shared_count(ph, s))
                        if c >= 1:
                            act.wait_ge(ksplit, ph.count(lambda o: SPLIT_STEPS * (c + o)))
                        nc.scalar.activation(k_f[:, :], shared_ps[:, :], ACT.Identity, bias=bk_sb[:, 0:1])\
                            .then_inc(shared_emptied, 1)
                    if s[0] == "send_max":
                        c, g = s[1:]
                        act.wait_ge(shared_filled, shared_count(ph, s))
                        if c >= 1:
                            act.wait_ge(max_in[g], ph.count(lambda o: 96 * (c + o)))
                        nc.scalar.activation(mx_t[:, g, :], shared_bf[0:3 * H // 2, 0:CH], ACT.Copy)\
                            .then_inc(shared_emptied, 1)
                    if s[0] == "transpose_o":
                        act.wait_ge(shared_filled, shared_count(ph, s))
                        nc.scalar.activation(o_nt[:, :], shared_ps[:, :], ACT.Copy).then_inc(shared_emptied, 1)

            phases(act, body)

        @block.vector
        def _(dve):
            dve.wait_ge(loaded, 16 * LOADS)
            w1_hi_f, w1_hi_r = w1_hi[:, :].bitcast(F32), w1_hi[:, :]
            nc.vector.memset(wr_hi[:, :].bitcast(F32), 0.0).then_inc(rows_cleared, 1)
            nc.vector.memset(wr_lo[:, :].bitcast(F32), 0.0).then_inc(rows_cleared, 1)
            nc.vector.tensor_copy(w1_hi_r, w1_f[:, :]).then_inc(weights_split, 1)
            nc.vector.tensor_copy(wqk_hi[:, :, :], wqk_f[:, :, :]).then_inc(weights_split, 1)
            nc.vector.tensor_scalar(bqs_sb[:, :], bq_sb[:, :], QSCALE, None, ALU.mult).then_inc(weights_split, 1)
            dve.wait_ge(rows_cleared, 2)
            nc.vector.tensor_copy(wr_hi[:, 0:E], wr_f[:, :]).then_inc(weights_split, 1)
            dve.wait_ge(weights_split, 4)
            nc.vector.tensor_tensor(wr_lo[:, 0:E], wr_f[:, :], wr_hi[:, 0:E].bitcast(F32), ALU.subtract)\
                .then_inc(weights_split, 1)
            nc.vector.tensor_tensor(w1_lo[:, :], w1_f[:, :], w1_hi_f, ALU.subtract).then_inc(weights_split, 1)
            nc.vector.tensor_tensor(wqk_lo[:, :, :], wqk_f[:, :, :], wqk_hi[:, :, :].bitcast(F32), ALU.subtract)\
                .then_inc(weights_split, 1)

            def body(ph):
                for s in steps(ph.c):
                    if s[0] == "down":
                        which, k, t, part = s[1:]
                        if part == 0:
                            continue
                        e, half = t // 2, t % 2
                        n = call(which, k)
                        acc = x1 if which == 1 else y_out
                        at = ph.count(lambda o: HSLOT * call(which, k + o) + t)
                        dve.wait_ge(down_filled, at + 1)
                        if e >= 1:
                            dve.wait_ge(down_added, at - 1)
                        elif half == 0:
                            dve.wait_ge(shared_emptied, shared_count(ph, ("bias_down", which, k)))
                        for tt in (2 * half, 2 * half + 1):
                            last = nc.vector.scalar_tensor_tensor(
                                out=acc[:, k % 2, tt, :], in0=down_ps[:, half, tt % 2, :],
                                scalar=gates[:, n % 2, tt, e:e + 1], in1=acc[:, k % 2, tt, :],
                                op0=ALU.mult, op1=ALU.add)
                        last.then_inc(down_added, 1)
                    if s[0] == "ln_stats":
                        which, k = s[1], s[2]
                        m = min(which, 1)
                        src = (x1, x_in, x2)[which]
                        if which == 0:
                            dve.wait_ge(down_added, ph.count(lambda o: 16 * call_ff1(k + o) + 16))
                        elif which == 1:
                            dve.wait_ge(x_loaded[k % 2], ph.count(lambda o: 16 * ((k + o) // 2 + 1)))
                        else:
                            dve.wait_ge(shared_emptied, shared_count(ph, ("project_o", k)))
                        for tt in range(TT):
                            nc.vector.bn_stats(stats[:, m, tt, :], src[:, k % 2, tt, :]).then_inc(stats_done[m], 1)
                        dve.wait_ge(stats_done[m], ln_count(ph, which, k, TT) + TT)
                        first = k == 0 and which < 2
                        if not first:
                            dve.wait_ge(rstd_done[m], ln_count(ph, which, k, 1))
                        hold(dve)
                        for tt in range(TT):
                            nc.vector.bn_aggr(mv[:, m, tt, :], stats[:, m, tt, :]).then_inc(moments_done[m], 1)
                    if s[0] == "ln_apply":
                        which, k = s[1], s[2]
                        m = min(which, 1)
                        src = (x1, x_in, x2)[which]
                        dve.wait_ge(rstd_done[m], ln_count(ph, which, k, 1) + 1)
                        dve.wait_ge(moments_done[m], ln_count(ph, which, k, TT) + TT)
                        if which == 0 and k >= 1:
                            dve.wait_ge(shared_filled, shared_count(ph, ("transpose_x", 0, k - 1)))
                        elif which == 2 or which == 1 and k >= 1:
                            dve.wait_ge(xf_hi_done, ph.count(lambda o: call(which, k + o)))
                        for tt in range(TT):
                            nc.vector.tensor_scalar(xn[:, m, tt, :], src[:, k % 2, tt, :], mv[:, m, tt, 0:1],
                                                    rstd[:, m, tt:tt + 1], ALU.subtract, ALU.mult)\
                                .then_inc(xn_done[m], 1)
                    if s[0] == "transpose_x" and s[1] == 0:
                        k = s[2]
                        dve.wait_ge(shared_emptied, shared_count(ph, s))
                        if k >= 1:
                            dve.wait_ge(shared_filled, shared_count(ph, ("project_k", k - 1)))
                        nc.vector.tensor_copy(xa_hi[:, :], xt[:, :]).then_inc(xsplit, 1)
                        dve.wait_ge(xsplit, ph.count(lambda o: 2 * (k + o) + 1))
                        nc.vector.tensor_tensor(xa_lo[:, :], xt[:, :], xa_hi[:, :].bitcast(F32), ALU.subtract)\
                            .then_inc(xsplit, 1)
                    if s[0] == "transpose_x" and s[1] > 0:
                        which, k = s[1], s[2]
                        n = call(which, k)
                        dve.wait_ge(xf_hi_done, ph.count(lambda o: call(which, k + o) + 1))
                        nc.vector.tensor_tensor(xf_lo[:, n % 2, :], shared_ps[:, :], xf_hi[:, n % 2, :].bitcast(F32),
                                                ALU.subtract).then_inc(shared_emptied, 1)
                    if s[0] == "gate":
                        which, k = s[1], s[2]
                        n = call(which, k)

                        def step(j):
                            dve.wait_ge(gate_step, ph.count(lambda o: GATE_STEPS * call(which, k + o) + j))

                        dve.wait_ge(shared_filled, shared_count(ph, s))
                        if n >= 1:
                            dve.wait_ge(gate_exp, ph.count(lambda o: call(which, k + o)))
                        nc.vector.tensor_copy(logit[:, :, :], shared_ps[:, 0:TT * E].rearrange("p (t e) -> p t e", e=E))\
                            .then_inc(shared_emptied, 1)
                        dve.wait_ge(shared_emptied, shared_count(ph, s))
                        nc.vector.tensor_reduce(out=top[:, :], in_=logit[:, :, :], op=ALU.max, axis=AX.X)\
                            .then_inc(gate_step, 1)
                        step(1)
                        nc.vector.tensor_tensor(below[:, :, :], logit[:, :, :],
                                                top[:, :].unsqueeze(2).broadcast_to([P, TT, E]), ALU.subtract)\
                            .then_inc(gate_step, 1)
                        other = logit[:, :, :].unsqueeze(2).broadcast_to([P, TT, E, E])
                        own = logit[:, :, :].unsqueeze(3).broadcast_to([P, TT, E, E])
                        nc.vector.tensor_tensor(beats[:, :, :, :], other, own, ALU.is_gt).then_inc(gate_step, 1)
                        nc.vector.tensor_tensor(ties[:, :, :, :], other, own, ALU.is_equal).then_inc(gate_step, 1)
                        step(4)
                        nc.vector.tensor_tensor(ties[:, :, :, :], ties[:, :, :, :],
                                                tri_sb[:, :, :].unsqueeze(1).broadcast_to([P, TT, E, E]), ALU.mult)\
                            .then_inc(gate_step, 1)
                    if s[0] == "gate_end":
                        which, k = s[1], s[2]
                        n = call(which, k)

                        def step(j):
                            dve.wait_ge(gate_step, ph.count(lambda o: GATE_STEPS * call(which, k + o) + j))

                        step(5)
                        nc.vector.tensor_tensor(beats[:, :, :, :], beats[:, :, :, :], ties[:, :, :, :], ALU.add)\
                            .then_inc(gate_step, 1)
                        step(6)
                        nc.vector.tensor_reduce(out=rank[:, :, :], in_=beats[:, :, :, :], op=ALU.add, axis=AX.X)\
                            .then_inc(gate_step, 1)
                        step(7)
                        dve.wait_ge(gate_exp, ph.count(lambda o: call(which, k + o) + 1))
                        nc.vector.scalar_tensor_tensor(out=chosen[:, :, :], in0=rank[:, :, :], scalar=1.5,
                                                       in1=expd[:, :, :], op0=ALU.is_lt, op1=ALU.mult)\
                            .then_inc(gate_step, 1)
                        step(8)
                        nc.vector.tensor_reduce(out=gsum[:, :], in_=chosen[:, :, :], op=ALU.add, axis=AX.X)\
                            .then_inc(gate_step, 1)
                        step(9)
                        nc.vector.reciprocal(grec[:, :], gsum[:, :]).then_inc(gate_step, 1)
                        step(10)
                        nc.vector.scalar_tensor_tensor(out=gates[:, n % 2, :, :], in0=chosen[:, :, :], scalar=0.5,
                                                       in1=grec[:, :].unsqueeze(2).broadcast_to([P, TT, E]),
                                                       op0=ALU.mult, op1=ALU.mult).then_inc(gates_done, 1)
                    if s[0] == "bias_down":
                        which, k = s[1], s[2]
                        res, acc = (x_in, x1) if which == 1 else (x2, y_out)
                        dve.wait_ge(shared_filled, shared_count(ph, s))
                        if which == 1 and k >= 2:
                            dve.wait_ge(x2_seeded, ph.count(lambda o: k + o - 1))
                        if which == 2 and k >= 2:
                            dve.wait_ge(out_stored[k % 2], ph.count(lambda o: 16 * ((k + o) // 2)))
                        nc.vector.tensor_tensor(acc[:, k % 2, :, :],
                                                shared_ps[:, :].rearrange("p (t d) -> p t d", d=D),
                                                res[:, k % 2, :, :], ALU.add).then_inc(shared_emptied, 1)
                    if s[0] == "project_q":
                        c = s[1]

                        def step(j):
                            dve.wait_ge(qsplit, ph.count(lambda o: SPLIT_STEPS * (c + o) + j))

                        dve.wait_ge(shared_emptied, shared_count(ph, s))
                        if c >= 1:
                            dve.wait_ge(qk_out, ph.count(lambda o: 96 * (c + o)))
                        nc.vector.tensor_copy(q_part[:, 0, :], q_f[:, :]).then_inc(qsplit, 1)
                        step(1)
                        nc.vector.tensor_tensor(q_rest[:, :], q_f[:, :], q_part[:, 0, :], ALU.subtract)\
                            .then_inc(qsplit, 1)
                        step(2)
                        nc.vector.tensor_copy(q_part[:, 1, :], q_rest[:, :]).then_inc(qsplit, 1)
                        step(3)
                        nc.vector.tensor_tensor(q_part[:, 2, :], q_rest[:, :], q_part[:, 1, :], ALU.subtract)\
                            .then_inc(qsplit, 1)
                    if s[0] == "project_v":
                        c = s[1]
                        dve.wait_ge(shared_filled, shared_count(ph, s))
                        if c == 0:
                            dve.wait_ge(cleared, 2)
                        if c >= 2:
                            dve.wait_ge(pv_filled, ph.count(lambda o: 4 * (c + o - 1)))
                        for tt in range(TT):
                            last = nc.vector.tensor_tensor(
                                v_st[c % 2][:, tt, :, 0:HD],
                                shared_ps[:, tt * D:(tt + 1) * D].rearrange("p (h d) -> p h d", d=HD),
                                bv_bc[:, :].rearrange("p (h d) -> p h d", d=HD), ALU.add)
                        last.then_inc(shared_emptied, 1)
                    if s[0] == "score_max":
                        c, h, b = s[1:]
                        dve.wait_ge(max_filled, ph.count(lambda o: 2 * H * (c + o) + 2 * h + b + 1))
                        if c >= 1 and h == 0 and b == 0:
                            dve.wait_ge(max_step, ph.count(lambda o: MAX_STEPS * (c + o - 1) + MAX_STEPS // 2 + 1))
                        if c + h >= 1:
                            dve.wait_ge(max_taken, ph.count(lambda o: 2 * H * (c + o) + 2 * h + b - 1))
                        hold(dve)
                        for i, cols in ((0, slice(0, P)), (1, slice(P, 3 * P))):
                            width = cols.stop - cols.start
                            last = nc.vector.tensor_tensor_reduce(
                                out=score_junk[:, b, cols], in0=score_ps[:, b, cols], in1=mask_sb[:, 2 * P - width:],
                                scale=1.0, scalar=-3e38, op0=ALU.add, op1=ALU.max,
                                accum_out=mx[:, 2 * b + i, h:h + 1])
                        last.then_inc(max_taken, 1)
                    if s[0] == "split_max":
                        c, g = s[1:]

                        def step(j):
                            dve.wait_ge(max_step, ph.count(lambda o: MAX_STEPS * (c + o) + MAX_STEPS // 2 * g + j))

                        dve.wait_ge(max_taken, ph.count(lambda o: 2 * H * (c + o) + H * (g + 1)))
                        flat = neg_mx[:, :, g, :, :].rearrange("p t a h -> p t (a h)")
                        rest = mx_rest[:, g, :, :]
                        nc.vector.tensor_scalar(neg_mx[:, :, g, :, :],
                                                mx[:, :, g * H // 2:(g + 1) * H // 2].rearrange(
                                                    "p t (h a) -> p t a h", a=2), -1.0, None,
                                                ALU.mult).then_inc(max_step, 1)
                        step(1)
                        if c >= 1:
                            dve.wait_ge(shared_filled, shared_count(ph, ("send_max", c - 1, g)))
                        nc.vector.tensor_copy(mx_part[:, :, g, 0, :], flat).then_inc(max_step, 1)
                        step(2)
                        nc.vector.tensor_tensor(rest, flat, mx_part[:, :, g, 0, :], ALU.subtract).then_inc(max_step, 1)
                        step(3)
                        nc.vector.tensor_copy(mx_part[:, :, g, 1, :], rest).then_inc(max_step, 1)
                        step(4)
                        nc.vector.tensor_tensor(mx_part[:, :, g, 2, :], rest, mx_part[:, :, g, 1, :], ALU.subtract)\
                            .then_inc(max_step, 1)
                    if s[0] == "normalise":
                        c, tt = s[1], s[2]
                        dve.wait_ge(shared_filled, shared_count(ph, s))
                        if tt == 0 and c >= 1:
                            dve.wait_ge(shared_filled, shared_count(ph, ("transpose_o", c - 1)))
                        o = shared_ps[:, :].rearrange("p (h w) -> p h w", w=32)
                        nc.vector.reciprocal(o_rec[:, :].unsqueeze(2), o[:, :, HD:HD + 1]).then_inc(rec_done, 1)
                        dve.wait_ge(rec_done, ph.count(lambda q: TT * (c + q) + tt + 1))
                        nc.vector.tensor_tensor(o_n[:, tt, :].rearrange("p (h d) -> p h d", d=HD), o[:, :, 0:HD],
                                                o_rec[:, :].unsqueeze(2).broadcast_to([P, H, HD]), ALU.mult)\
                            .then_inc(shared_emptied, 1)
                    if s[0] == "project_o":
                        c = s[1]
                        dve.wait_ge(shared_filled, shared_count(ph, s))
                        dve.wait_ge(x2_seeded, ph.count(lambda o: c + o + 1))
                        nc.vector.tensor_tensor(x2[:, c % 2, :, :], shared_ps[:, :].rearrange("p (t d) -> p t d", d=D),
                                                x2[:, c % 2, :, :], ALU.add).then_inc(shared_emptied, 1)

            phases(dve, body)

        @block.tensor
        def _(pe):
            pe.wait_ge(loaded, 16 * LOADS)
            pe.wait_ge(weights_split, 7)
            mm, tr = nc.tensor.matmul, nc.tensor.transpose

            def three(out, hi, lo, x_hi, x_lo):
                mm(out, hi, x_hi, start=True, stop=False)
                mm(out, hi, x_lo, start=False, stop=False)
                return mm(out, lo, x_hi, start=False, stop=True)

            def body(ph):
                for s in steps(ph.c):
                    if s[0] in SHARED and SHARED_AT[s] > 0:
                        pe.wait_ge(shared_emptied, shared_count(ph, s) - 1)
                    if s[0] == "up":
                        which, k, t = s[1:]
                        n = call(which, k)
                        tile = ph.count(lambda o: HSLOT * call(which, k + o) + t)
                        if t == 0:
                            pe.wait_ge(shared_emptied, shared_count(ph, ("transpose_x", which, k)))
                        if HSLOT * n + t >= 2:
                            pe.wait_ge(up_relued, tile - 1)
                        w = slice(t * P, (t + 1) * P)
                        three(up_ps[:, t % 2, :], w1_hi[:, w], w1_lo[:, w], xf_hi[:, n % 2, :], xf_lo[:, n % 2, :])\
                            .then_inc(up_filled, 1)
                    if s[0] == "down":
                        which, k, t, part = s[1:]
                        e, half = t // 2, t % 2
                        at = ph.count(lambda o: HSLOT * call(which, k + o) + t)
                        if half == 0 and part == 0:
                            pe.wait_ge(up_relued, at + 2)
                        if part == 0 and HSLOT * call(which, k) + t >= 2:
                            pe.wait_ge(down_added, at - 1)
                        for tt in (2 * half + part,):
                            for j in range(2):
                                last = mm(down_ps[:, half, tt % 2, :], hid[:, (2 * e + j) % 4, tt * P:(tt + 1) * P],
                                          w2_sb[:, e, j, :], start=j == 0, stop=j == 1)
                        if part == 1:
                            last.then_inc(down_filled, 1)
                    if s[0] == "transpose_x":
                        which, k = s[1], s[2]
                        m = min(which, 1)
                        pe.wait_ge(xn_done[m], ln_count(ph, which, k, TT) + TT)
                        for tt in range(TT):
                            last = tr(shared_ps[:, tt * P:(tt + 1) * P], xn[:, m, tt, :], id_f[:, :])
                        last.then_inc(shared_filled, 1)
                    if s[0] == "route":
                        n = call(s[1], s[2])
                        three(shared_ps[:, :], wr_hi[:, :], wr_lo[:, :], xf_hi[:, n % 2, :], xf_lo[:, n % 2, :])\
                            .then_inc(shared_filled, 1)
                    if s[0] == "gate":
                        hold(pe)
                        for tt in range(TT):
                            last = tr(shared_ps[:, tt * E:(tt + 1) * E], logit_t[:, tt * P:(tt + 1) * P],
                                      id_f[0:E, 0:E])
                        last.then_inc(shared_filled, 1)
                    if s[0] == "transpose_g":
                        which, k = s[1], s[2]
                        n = call(which, k)
                        pe.wait_ge(gates_done, ph.count(lambda o: call(which, k + o) + 1))
                        hold(pe)
                        for tt in range(TT):
                            last = tr(shared_ps[0:E, tt * P:(tt + 1) * P], gates[:, n % 2, tt, :], id_f[:, :])
                        last.then_inc(shared_filled, 1)
                    if s[0] == "bias_down":
                        for tt in range(TT):
                            last = mm(shared_ps[:, tt * D:(tt + 1) * D], gates_t[:, tt * P:(tt + 1) * P], b2_sb[:, :],
                                      start=True, stop=True)
                        last.then_inc(shared_filled, 1)
                    if s[0] in ("project_q", "project_k"):
                        c, j = s[1], int(s[0] == "project_k")
                        pe.wait_ge(xsplit, ph.count(lambda o: 2 * (c + o) + 2))
                        three(shared_ps[:, :], wqk_hi[:, j, :], wqk_lo[:, j, :], xa_hi[:, :], xa_lo[:, :])\
                            .then_inc(shared_filled, 1)
                    if s[0] == "project_v":
                        for tt in range(TT):
                            last = mm(shared_ps[:, tt * D:(tt + 1) * D], xt[:, tt * P:(tt + 1) * P], wv_sb[:, :],
                                      start=True, stop=True)
                        last.then_inc(shared_filled, 1)
                    if s[0] == "score_max":
                        c, h, b = s[1:]
                        if h == 0:
                            if b == 0:
                                pe.wait_ge(qk_in, ph.count(lambda o: 64 * (c + o + 1)))
                            if c >= 1:
                                pe.wait_ge(exp_done, ph.count(lambda o: 2 * H * (c + o) - 1 + b))
                        else:
                            pe.wait_ge(max_taken, ph.count(lambda o: 2 * H * (c + o) + 2 * h + b - 1))
                        rows = slice(64 * (h % 2), 64 * (h % 2) + ROWS_A)
                        q, k = q_st[c % 2], k_st[c % 2]
                        for i, cols in ((0, slice(0, P)), (1, slice(P, 3 * P))):
                            i0 = b * T + i * P
                            last = mm(score_ps[:, b, cols], q[rows, h // 2, i0:i0 + P],
                                      k[rows, h // 2, b * T:i0 + P], start=True, stop=True)
                        last.then_inc(max_filled, 1)
                    if s[0] == "send_max":
                        c, g = s[1:]
                        pe.wait_ge(max_step, ph.count(lambda o: MAX_STEPS * (c + o) + MAX_STEPS // 2 * (g + 1)))
                        hold(pe)
                        for tt in range(TT):
                            last = tr(shared_bf[0:3 * H // 2, tt * P:(tt + 1) * P], mx_part[:, tt, g, :, :],
                                      id_b[:, :])
                        last.then_inc(shared_filled, 1)
                    if s[0] == "score_exp":
                        c, h, b = s[1:]
                        if h % (H // 2) == 0 and b == 0:
                            pe.wait_ge(max_in[h // (H // 2)], ph.count(lambda o: 96 * (c + o + 1)))
                        if h == 0:
                            if b == 0:
                                pe.wait_ge(max_taken, ph.count(lambda o: 2 * H * (c + o + 1)))
                        else:
                            pe.wait_ge(exp_done, ph.count(lambda o: 2 * H * (c + o) + 2 * h + b - 1))
                        rows = slice(64 * (h % 2), 64 * (h % 2) + ROWS_B)
                        q, k = q_st[c % 2], k_st[c % 2]
                        for j, cols in ((0, slice(0, 2 * P)), (1, slice(2 * P, 3 * P))):
                            j0 = b * T + j * P
                            last = mm(score_ps[:, b, cols], k[rows, h // 2, j0:j0 + P],
                                      q[rows, h // 2, j0:(b + 1) * T], start=True, stop=True)
                        last.then_inc(exp_filled, 1)
                    if s[0] == "pv":
                        c, g = s[1], s[2]
                        pe.wait_ge(causal_done, ph.count(lambda o: 2 * H * (c + o) + 8 * g + 8))
                        if 4 * c + g >= 1:
                            pe.wait_ge(o_copied, ph.count(lambda o: 4 * (c + o) + g))
                        for b in range(2):
                            for j in range(2):
                                for hh in range(4):
                                    h = 4 * g + hh
                                    p = prob[:, h % 8, b, 0:2, :] if j == 0 else prob[:, h % 8, b, 2:3, :]
                                    last = mm(o_ps[32 * hh:32 * hh + 32, b * T + j * P:(b + 1) * T],
                                              v_st[c % 2][:, 2 * b + j, h, :], p, start=j == 0, stop=j == 1)
                        last.then_inc(pv_filled, 1)
                    if s[0] == "normalise":
                        c, tt = s[1], s[2]
                        if tt == 0:
                            pe.wait_ge(o_copied, ph.count(lambda o: 4 * (c + o) + 4))
                        for g in range(4):
                            last = tr(shared_ps[:, g * P:(g + 1) * P], o_t[:, g, tt * P:(tt + 1) * P], id_f[:, :])
                        last.then_inc(shared_filled, 1)
                    if s[0] == "transpose_o":
                        for tt in range(TT):
                            last = tr(shared_ps[:, tt * P:(tt + 1) * P], o_n[:, tt, :], id_f[:, :])
                        last.then_inc(shared_filled, 1)
                    if s[0] == "project_o":
                        for tt in range(TT):
                            last = mm(shared_ps[:, tt * D:(tt + 1) * D], o_nt[:, tt * P:(tt + 1) * P], wo_sb[:, :],
                                      start=True, stop=True)
                        last.then_inc(shared_filled, 1)

            phases(pe, body)


def kernel(L0_attn_x, L0_attn_Wq, L0_attn_bq, L0_attn_Wk, L0_attn_bk, L0_attn_Wv, L0_attn_bv, L0_attn_Wo,
           L0_attn_bo, L0_ffn_Wr, L0_ffn_br, L0_ffn_W1, L0_ffn_b1, L0_ffn_W2, L0_ffn_b2):
    import numpy as np
    import ml_dtypes
    import concourse.bacc as bacc
    from concourse.bass_utils import run_bass_kernel_spmd

    lay = np.ascontiguousarray
    a = {
        "x": lay(np.asarray(L0_attn_x).reshape(B * T, D)),
        "wq": lay(np.asarray(L0_attn_Wq).T), "bq": lay(np.asarray(L0_attn_bq).reshape(D, 1)),
        "wk": lay(np.asarray(L0_attn_Wk).T), "bk": lay(np.asarray(L0_attn_bk).reshape(D, 1)),
        "wv": lay(np.asarray(L0_attn_Wv).T), "bv": lay(np.asarray(L0_attn_bv)),
        "wo": lay(np.asarray(L0_attn_Wo).T), "bo": lay(np.asarray(L0_attn_bo)),
        "wr": lay(np.asarray(L0_ffn_Wr)), "br": lay(np.asarray(L0_ffn_br).reshape(E, 1)),
        "w1": lay(np.asarray(L0_ffn_W1).transpose(1, 0, 2).reshape(D, E * HID)),
        "b1": lay(np.asarray(L0_ffn_b1).reshape(E * 2, P).T),
        "w2": lay(np.asarray(L0_ffn_W2).reshape(E, 2, P, D).transpose(2, 0, 1, 3)),
        "b2": lay(np.asarray(L0_ffn_b2)),
    }
    bf = ml_dtypes.bfloat16
    a["ident"] = np.eye(P, dtype=np.float32)
    a["ident_b"] = np.eye(P, dtype=bf)
    a["mask"] = np.concatenate([np.zeros((P, P), np.float32), np.triu(np.full((P, P), -1e30, np.float32), 1)], 1)
    a["tri"] = np.tril(np.ones((E, E), np.float32), -1).reshape(E * E)
    pos = np.tile(np.arange(T, dtype=np.float32), 2)
    rows_q = np.zeros((64 - ROWS_QK, H // 2, CH), np.float32)
    rows_k = np.zeros((64 - ROWS_QK, H // 2, CH), np.float32)
    rows_q[0], rows_q[1] = 1.0, -pos
    rows_k[0], rows_k[1:5] = pos, 1.0
    masks = [(block * P + first, length) for block in range(2) for first, length in MASKED]
    for r, (first, length) in enumerate(masks, ROWS_M - ROWS_QK):
        rows_q[r] = (pos >= first) & (pos < first + length // 2)
        rows_k[r] = np.where((pos >= first + length // 2) & (pos < first + length), -1e30, 0.0)
    a["qrows"], a["krows"] = rows_q.astype(bf), rows_k.astype(bf)

    nc = bacc.Bacc("TRN2", target_bir_lowering=False, num_devices=1)
    arrays, args = {}, []
    for name, arr in a.items():
        arrays[name + "_dram"] = arr
        args.append(nc.dram_tensor(name + "_dram", arr.shape, mybir.dt.from_np(arr.dtype), kind="ExternalInput").ap())
    for name in ("zq", "zk"):
        args.append(nc.dram_tensor(name, [2, P, PIECES, CH], BF16, kind="Internal").ap())
    args.append(nc.dram_tensor("out_dram", [B * T, D], F32, kind="ExternalOutput").ap())
    macaron_kernel(nc, *args)
    r = run_bass_kernel_spmd(nc, [arrays], core_ids=[0])
    return r.results[0]["out_dram"].reshape(B, T, D)
```

```python
import concourse.bass as bass
from concourse import mybir
from contextlib import ExitStack

F32 = mybir.dt.float32
F32R = mybir.dt.float32r
BF16 = mybir.dt.bfloat16
ALU = mybir.AluOpType
ACT = mybir.ActivationFunctionType
AX = mybir.AxisListType

P = 128
D = 128
T = 256
B = 32
CH = 512
TT = CH // P
NC = B * T // CH
H, HD = 16, 8
E, HID = 8, 256
EPS = 1e-5
QSCALE = 1.0 / float(HD) ** 0.5
PIECES = 6
ROWS_QK = PIECES * HD
ROWS_A = ROWS_QK + 2
ROWS_M = ROWS_A + 3
MASKED = ((0, 128), (0, 64), (64, 64))
ROWS_B = ROWS_M + 2 * len(MASKED)
HSLOT = 16

FIRST, LOOP_FROM, LOOP_TO, LAST = -2, 2, 12, NC + 1


def call_ff1(k):
    return k if k < 3 else 2 * k - 3


def call_ff2(k):
    return 2 * k + 4 if k < NC - 3 else NC + k


def up_at(which, k, t):
    if (which, k) == (1, 0):
        return t - 36 if t < 4 else t - 34
    if which == 1:
        return (0, t - 16, 2 * t)[k] if k < 3 else 32 * (k - 2) + t
    return 32 * (k + 1) + 16 + (2 * t if spread(which, k) else t)


def spread(which, k):
    return (which, k) == (1, 2) or which == 2 and NC - 4 <= k < NC - 1


def down_at(which, k, t):
    return t - 32 if (which, k) == (1, 0) else up_at(which, k, t) + 2 + spread(which, k)


TILES = [(which, k, t) for which in (1, 2) for k in range(NC) for t in range(HSLOT)]
UP_AT = {up_at(*tile): tile for tile in TILES}
DOWN_AT = {down_at(*tile): tile for tile in TILES}


def steps(c):
    def there(k):
        return 0 <= k < NC

    places = [(k, place) for k in range(17, 32) for place in range(3)]
    exp_at = [places[u * len(places) // (2 * H)] for u in range(2 * H)]
    out = []
    if there(c + 3) and c + 3 >= 2:
        out.append(("load_x", c + 3))
    beside = []
    if there(c - 2):
        beside += [(("store", c - 2), 18 if spread(2, c - 2) else 2, 2)]
    if there(c - 1):
        m = c - 1
        beside += [(("pv", m, 3), 2, 0), (("take_pv", m, 3), 2, 1),
                   (("normalise", m, 0), 3, 2), (("normalise", m, 1), 4, 2),
                   (("normalise", m, 2), 5, 2), (("normalise", m, 3), 6, 2),
                   (("transpose_o", m), 7, 2), (("project_o", m), 8, 2), (("ln_stats", 2, m), 9, 2),
                   (("ln_apply", 2, m), 11, 0), (("transpose_x", 2, m), 12, 2), (("route", 2, m), 14, 1),
                   (("gate", 2, m), 15, 1), (("gate_end", 2, m), 15, 2), (("transpose_g", 2, m), 18, 0),
                   (("bias_down", 2, m), 18, 1)]
    if there(c):
        beside += [(("split_max", c, 0), 8, 0), (("send_max", c, 0), 10, 2),
                   (("split_max", c, 1), 17, 0), (("send_max", c, 1), 19, 1)]
    if there(c + 1):
        m = c + 1
        beside += [(("ln_stats", 0, m), 18, 2), (("ln_apply", 0, m), 19, 2), (("seed_x2", m), 20, 0),
                   (("transpose_x", 0, m), 21, 1),
                   (("project_q", m), 22, 2), (("project_k", m), 23, 2), (("project_v", m), 24, 2)]
        beside += [(("split_k", m, n), 24 + (n if c < LOOP_TO else n // 2), 0) for n in range(4)]
    for m, first in {-2: [(0, 20)], -1: [(1, 0), (2, 20)]}.get(c, [(c + 3, 20)]):
        if there(m):
            beside += [(("ln_stats", 1, m), first, 2), (("ln_apply", 1, m), first + 4, 0),
                       (("transpose_x", 1, m), first + 6, 1), (("route", 1, m), first + 7, 1),
                       (("gate", 1, m), first + 8, 1), (("gate_end", 1, m), first + 9, 1),
                       (("transpose_g", 1, m), first + 10, 2), (("bias_down", 1, m), first + 11, 2)]
    if c == -2:
        beside += [(("split_router",), 25, 0)] + [(("split_w1", n), 27 + n // 2, 0) for n in range(4)]
    if c == -1:
        beside += [(("split_qk",), 12, 0)]

    for k in range(32):
        def others(place):
            out.extend(s for s, at, p in beside if (at, p) == (k, place))

        def score(place):
            if there(c) and k < H and place != 1:
                out.append(("score_max", c, k, place // 2))
            if there(c) and (k, place) in exp_at:
                u = exp_at.index((k, place))
                out.append(("score_exp", c, u // 2, u % 2))
                if u % 8 == 4 and u > 8:
                    out.append(("pv", c, u // 8 - 1))
                if u % 8 == 5 and u > 8:
                    out.append(("take_pv", c, u // 8 - 1))

        others(0)
        up, down = UP_AT.get(32 * c + k), DOWN_AT.get(32 * c + k)
        if up and down:
            out.append(("up",) + up)
        score(0)
        if up and not down:
            out.append(("up",) + up)
        if down:
            out.append(("down",) + down + (0,))
        score(1)
        others(1)
        if down:
            out.append(("down",) + down + (1,))
        score(2)
        others(2)
    return out


SHARED = ("normalise", "transpose_o", "project_o", "transpose_x", "route", "gate", "transpose_g",
          "bias_down", "send_max", "project_q", "project_k", "project_v")
SHARED_AT = {s: n for n, s in enumerate(s for c in range(FIRST, LAST + 1) for s in steps(c) if s[0] in SHARED)}


def macaron_kernel(nc, x, wq, bq, wk, bk, wv, bv, wo, bo, wr, br, w1, b1, w2, b2,
                   ident, ident_b, mask, tri, qrows, krows, zq, zk, out):
    x_v = x.rearrange("(c t p) d -> c p t d", t=TT, p=P)
    out_v = out.rearrange("(c t p) d -> c p t d", t=TT, p=P)

    with ExitStack() as ctx:
        def sb(name, shape, dt=F32):
            return ctx.enter_context(nc.sbuf_tensor(name, shape, dt))

        def sem(name):
            return ctx.enter_context(nc.semaphore(name))

        w1_f = sb("w1_f", [P, E * HID])
        w1_hi = sb("w1_hi", [P, E * HID], F32R)
        w1_lo = sb("w1_lo", [P, E * HID], F32R)
        w2_sb = sb("w2_sb", [P, E, 2, D])
        b1_sb = sb("b1_sb", [P, E * 2])
        b2_sb = sb("b2_sb", [E, D])
        wr_f = sb("wr_f", [P, E])
        wr_hi = sb("wr_hi", [P, P], F32R)
        wr_lo = sb("wr_lo", [P, P], F32R)
        br_sb = sb("br_sb", [E, 1])
        logit_t = sb("logit_t", [E, CH])
        wqk_f = sb("wqk_f", [P, 2, D])
        wqk_hi = sb("wqk_hi", [P, 2, D], F32R)
        wqk_lo = sb("wqk_lo", [P, 2, D], F32R)
        wv_sb = sb("wv_sb", [P, D])
        wo_sb = sb("wo_sb", [P, D])
        bq_sb = sb("bq_sb", [P, 1])
        bqs_sb = sb("bqs_sb", [P, 1])
        bk_sb = sb("bk_sb", [P, 1])
        bv_bc = sb("bv_bc", [P, D])
        bo_bc = sb("bo_bc", [P, D])
        id_f = sb("id_f", [P, P])
        id_b = sb("id_b", [P, P], BF16)
        mask_sb = sb("mask_sb", [P, 2 * P])
        score_junk = sb("score_junk", [P, 2, 3 * P], BF16)
        tri_sb = sb("tri_sb", [P, E, E])
        minus_half = sb("minus_half", [P, TT])
        x_in = sb("x_in", [P, 2, TT, D])
        x1 = sb("x1", [P, 2, TT, D])
        x2 = sb("x2", [P, 2, TT, D])
        y_out = sb("y_out", [P, 2, TT, D])
        stats = sb("stats", [P, 2, TT, 6])
        mv = sb("mv", [P, 2, TT, 2])
        var_eps = sb("var_eps", [P, 2, TT])
        rstd = sb("rstd", [P, 2, TT])
        xn = sb("xn", [P, 2, TT, D])
        xt = sb("xt", [P, CH])
        xa_hi = sb("xa_hi", [P, CH], F32R)
        xa_lo = sb("xa_lo", [P, CH], F32R)
        xf_hi = sb("xf_hi", [P, 2, CH], F32R)
        xf_lo = sb("xf_lo", [P, 2, CH], F32R)
        logit = sb("logit", [P, TT, E])
        top = sb("top", [P, TT])
        below = sb("below", [P, TT, E])
        expd = sb("expd", [P, TT, E])
        beats = sb("beats", [P, TT, E, E])
        ties = sb("ties", [P, TT, E, E])
        rank = sb("rank", [P, TT, E])
        chosen = sb("chosen", [P, TT, E])
        gsum = sb("gsum", [P, TT])
        grec = sb("grec", [P, TT])
        gates = sb("gates", [P, 2, TT, E])
        gates_t = sb("gates_t", [E, CH])
        hid = sb("hid", [P, 4, CH])
        q_f = sb("q_f", [P, CH])
        k_f = sb("k_f", [P, CH])
        q_rest = sb("q_rest", [P, CH])
        k_rest = sb("k_rest", [P, CH])
        q_part = sb("q_part", [P, 3, CH], BF16)
        k_part = sb("k_part", [P, 3, CH], BF16)
        q_st = [sb(f"q_st{i}", [P, H // 2, CH], BF16) for i in range(2)]
        k_st = [sb(f"k_st{i}", [P, H // 2, CH], BF16) for i in range(2)]
        v_st = [sb(f"v_st{i}", [P, TT, H, 32]) for i in range(2)]
        mx = sb("mx", [P, TT, H])
        neg_mx = sb("neg_mx", [P, TT, 2, 2, H // 4])
        mx_rest = sb("mx_rest", [P, 2, TT, H // 2])
        mx_part = sb("mx_part", [P, TT, 2, 3, H // 2], BF16)
        mx_t = sb("mx_t", [3 * H // 2, 2, CH], BF16)
        prob = sb("prob", [P, 8, 2, 3, P])
        o_t = sb("o_t", [P, 4, CH])
        o_rec = sb("o_rec", [P, H])
        o_n = sb("o_n", [P, TT, D])
        o_nt = sb("o_nt", [P, CH])

        up_ps = ctx.enter_context(nc.psum_tensor("up_ps", [P, 2, CH], F32))
        down_ps = ctx.enter_context(nc.psum_tensor("down_ps", [P, 2, TT, D], F32))
        score_ps = ctx.enter_context(nc.psum_tensor("score_ps", [P, 2, CH], F32))
        o_ps = ctx.enter_context(nc.psum_tensor("o_ps", [P, CH], F32))
        shared_ps = ctx.enter_context(nc.psum_tensor("shared_ps", [P, CH], F32))
        shared_bf = shared_ps[:, :].bitcast(BF16)

        router_loaded = sem("router_loaded")
        experts_loaded = sem("experts_loaded")
        rest_loaded = sem("rest_loaded")
        router_split = sem("router_split")
        w1_hi_done = sem("w1_hi_done")
        w1_split = sem("w1_split")
        qk_split = sem("qk_split")
        rows_cleared = sem("rows_cleared")
        cleared = sem("cleared")
        x_loaded = [sem(f"x_loaded{i}") for i in range(2)]
        out_stored = [sem(f"out_stored{i}") for i in range(2)]
        up_filled = sem("up_filled")
        up_relued = sem("up_relued")
        down_filled = sem("down_filled")
        down_added = sem("down_added")
        stats_done = [sem(f"stats_done{i}") for i in range(2)]
        moments_done = [sem(f"moments_done{i}") for i in range(2)]
        var_done = [sem(f"var_done{i}") for i in range(2)]
        rstd_done = [sem(f"rstd_done{i}") for i in range(2)]
        xn_done = [sem(f"xn_done{i}") for i in range(2)]
        xsplit = sem("xsplit")
        xf_hi_done = sem("xf_hi_done")
        shared_filled = sem("shared_filled")
        shared_emptied = sem("shared_emptied")
        gate_step = sem("gate_step")
        gates_done = sem("gates_done")
        gate_exp = sem("gate_exp")
        qsplit = sem("qsplit")
        ksplit = sem("ksplit")
        qk_out = sem("qk_out")
        qk_in = sem("qk_in")
        max_filled = sem("max_filled")
        max_taken = sem("max_taken")
        max_step = sem("max_step")
        max_in = [sem(f"max_in{g}") for g in range(2)]
        exp_filled = sem("exp_filled")
        exp_done = sem("exp_done")
        causal_done = sem("causal_done")
        pv_filled = sem("pv_filled")
        o_copied = sem("o_copied")
        rec_done = sem("rec_done")
        held = sem("held")
        x2_seeded = sem("x2_seeded")

        ROUTER_LOADS, EXPERT_LOADS, REST_LOADS = 5, 3, 18
        GATE_STEPS, SPLIT_STEPS, MAX_STEPS = 10, 4, 10

        block = ctx.enter_context(nc.Block())

        class Phase:

            def __init__(self, c, i=None):
                self.c, self.i = c, i

            def count(self, f):
                if self.i is None:
                    return f(0)
                for n in range(2, (LOOP_TO - LOOP_FROM) // 2):
                    assert f(2 * n) == f(0) + n * (f(2) - f(0))
                return f(0) + self.i * (f(2) - f(0))

        def phases(eng, body):
            for c in range(FIRST, LOOP_FROM):
                body(Phase(c))
            with eng.Fori(0, (LOOP_TO - LOOP_FROM) // 2) as i:
                for c in range(LOOP_FROM, LOOP_FROM + 2):
                    body(Phase(c, i))
            for c in range(LOOP_TO, LAST + 1):
                body(Phase(c))

        def shared_count(ph, s):
            def f(o):
                at = (s[0], s[1] + o, s[2]) if s[0] in ("normalise", "send_max") else s[:-1] + (s[-1] + o,)
                return SHARED_AT[at] + 1
            return ph.count(f)

        def call(which, k):
            return call_ff1(k) if which == 1 else call_ff2(k)

        def hold(eng):
            eng.sem_inc(held, 1)

        def ln_count(ph, which, k, per):
            return ph.count(lambda o: per * (k + o if which == 0 else call(which, k + o)))

        def max_bank(h, b):
            u = 2 * h + b
            n = u % 2 if u < 6 else (u - 7) % 3
            return o_ps if n == 2 else score_ps[:, n, :]

        @block.sync
        def _(sp):
            sp.dma_start(x_in[:, 0, :, :], x_v[0]).then_inc(x_loaded[0], 16)
            for dst, src in ((id_f[:, :], ident), (wr_f[:, :], wr), (br_sb[:, :], br),
                             (tri_sb[:, :, :].rearrange("p e f -> p (e f)"), tri.partition_broadcast(P)),
                             (b2_sb[:, :], b2)):
                sp.dma_start(dst, src).then_inc(router_loaded, 16)
            for dst, src in ((w1_f[:, :], w1), (b1_sb[:, :], b1), (w2_sb[:, :, :, :], w2)):
                sp.dma_start(dst, src).then_inc(experts_loaded, 16)
            sp.dma_start(x_in[:, 1, :, :], x_v[1]).then_inc(x_loaded[1], 16)
            for dst, src in ((wqk_f[:, 0, :], wq), (wqk_f[:, 1, :], wk), (wv_sb[:, :], wv), (wo_sb[:, :], wo),
                             (bq_sb[:, :], bq), (bk_sb[:, :], bk), (bv_bc[:, :], bv.partition_broadcast(P)),
                             (bo_bc[:, :], bo.partition_broadcast(P)), (id_b[:, :], ident_b),
                             (mask_sb[:, :], mask)):
                sp.dma_start(dst, src).then_inc(rest_loaded, 16)
            for st, rows in ((q_st, qrows), (k_st, krows)):
                for i in range(2):
                    for a in range(2):
                        sp.dma_start(st[i][64 * a + ROWS_QK:64 * a + 64, :, :], rows).then_inc(rest_loaded, 16)

            def body(ph):
                for s in steps(ph.c):
                    if s[0] == "load_x":
                        k = s[1]
                        sp.wait_ge(shared_emptied, shared_count(ph, ("bias_down", 1, k - 2)))
                        hold(sp)
                        sp.dma_start(x_in[:, k % 2, :, :], x_v[ph.count(lambda o: k + o)])\
                            .then_inc(x_loaded[k % 2], 16)
                    if s[0] == "store":
                        k = s[1]
                        sp.wait_ge(down_added, ph.count(lambda o: 16 * call_ff2(k + o) + 16))
                        hold(sp)
                        sp.dma_start(out_v[ph.count(lambda o: k + o)], y_out[:, k % 2, :, :])\
                            .then_inc(out_stored[k % 2], 16)
                    if s[0] == "send_max":
                        c, g = s[1:]
                        sp.wait_ge(shared_emptied, shared_count(ph, s))
                        hold(sp)
                        n = H // 4
                        for a in range(2):
                            for piece in range(3):
                                row = 64 * a + ROWS_A + piece
                                src = (2 * piece + a) * n
                                sp.dma_start(q_st[c % 2][row:row + 1, g * n:(g + 1) * n, :], mx_t[src:src + n, g, :])\
                                    .then_inc(max_in[g], 16)
                    if s[0] == "project_v":
                        c = s[1]
                        sp.wait_ge(qsplit, ph.count(lambda o: SPLIT_STEPS * (c + o + 1)))
                        hold(sp)
                        for z, part, dup in ((zq, q_part, False), (zk, k_part, True)):
                            if dup:
                                sp.wait_ge(ksplit, ph.count(lambda o: SPLIT_STEPS * (c + o + 1)))
                                hold(sp)
                                src = (part[:, 0:1, :].broadcast_to([P, 3, CH]),
                                       part[:, 1:2, :].broadcast_to([P, 2, CH]), part[:, 2:3, :])
                            else:
                                src = (part[:, 0:3, :], part[:, 0:2, :], part[:, 0:1, :])
                            for (r0, r1), sr in zip(((0, 3), (3, 5), (5, 6)), src):
                                sp.dma_start(z[c % 2, :, r0:r1, :], sr).then_inc(qk_out, 16)
                        sp.wait_ge(qk_out, ph.count(lambda o: 96 * (c + o + 1)))
                        hold(sp)
                        if c >= 2:
                            sp.wait_ge(exp_filled, ph.count(lambda o: 2 * H * (c + o - 1)))
                            hold(sp)
                        for z, st in ((zq, q_st), (zk, k_st)):
                            zr = z[c % 2].rearrange("(t a d) r n -> a (d r) t n", a=2, d=HD)
                            for a in range(2):
                                sp.dma_start(st[c % 2][64 * a:64 * a + ROWS_QK, :, :], zr[a]).then_inc(qk_in, 16)

            phases(sp, body)
            for k in range(2):
                sp.wait_ge(out_stored[k], 16 * NC // 2)

        @block.gpsimd
        def _(pool):
            for st in v_st:
                nc.gpsimd.memset(st[:, :, :, :], 0.0)
            nc.gpsimd.memset(minus_half[:, :], -0.5).then_inc(cleared, 1)
            pool.wait_ge(cleared, 1)
            for st in v_st:
                last = nc.gpsimd.memset(st[:, :, :, HD:HD + 1], 1.0)
            last.then_inc(cleared, 1)

            def body(ph):
                for s in steps(ph.c):
                    if s[0] == "ln_stats":
                        which, k = s[1], s[2]
                        m = min(which, 1)
                        pool.wait_ge(moments_done[m], ln_count(ph, which, k, TT) + TT)
                        hold(pool)
                        nc.gpsimd.tensor_scalar(var_eps[:, m, :], mv[:, m, :, 1], EPS, None, ALU.add)\
                            .then_inc(var_done[m], 1)
                        pool.wait_ge(var_done[m], ln_count(ph, which, k, 1) + 1)
                        nc.gpsimd.tensor_tensor(rstd[:, m, :], var_eps[:, m, :], minus_half[:, :], ALU.pow)\
                            .then_inc(rstd_done[m], 1)
                    if s[0] == "seed_x2":
                        c = s[1]
                        if c == 0:
                            pool.wait_ge(rest_loaded, 16 * REST_LOADS)
                        pool.wait_ge(down_added, ph.count(lambda o: 16 * call_ff1(c + o) + 16))
                        if c >= 2:
                            pool.wait_ge(shared_emptied, shared_count(ph, ("bias_down", 2, c - 2)))
                        nc.gpsimd.tensor_tensor(x2[:, c % 2, :, :], x1[:, c % 2, :, :],
                                                bo_bc[:, :].unsqueeze(1).broadcast_to([P, TT, D]), ALU.add)\
                            .then_inc(x2_seeded, 1)
                    if s[0] == "split_k":
                        c, n = s[1:]
                        if n == 0:
                            pool.wait_ge(shared_emptied, shared_count(ph, ("project_k", c)))
                            if c >= 1:
                                pool.wait_ge(qk_out, ph.count(lambda o: 96 * (c + o)))
                        else:
                            pool.wait_ge(ksplit, ph.count(lambda o: SPLIT_STEPS * (c + o) + n))
                        if n % 2 == 0:
                            hold(pool)
                            nc.gpsimd.tensor_copy(k_part[:, n // 2, :], (k_f if n == 0 else k_rest)[:, :])\
                                .then_inc(ksplit, 1)
                        elif n == 1:
                            nc.gpsimd.tensor_tensor(k_rest[:, :], k_f[:, :], k_part[:, 0, :], ALU.subtract)\
                                .then_inc(ksplit, 1)
                        else:
                            nc.gpsimd.tensor_tensor(k_part[:, 2, :], k_rest[:, :], k_part[:, 1, :], ALU.subtract)\
                                .then_inc(ksplit, 1)
                    if s[0] == "score_exp":
                        c, h, b = s[1:]
                        pool.wait_ge(exp_done, ph.count(lambda o: 2 * H * (c + o) + 2 * h + b + 1))
                        hold(pool)
                        diag = prob[:, h % 8, b, 0:3:2, :]
                        nc.gpsimd.affine_select(out=diag, in_=diag, compare_op=ALU.is_ge, fill=0.0, base=0,
                                                pattern=[[0, 2], [1, P]], channel_multiplier=-1)\
                            .then_inc(causal_done, 1)

            phases(pool, body)

        @block.scalar
        def _(act):
            def body(ph):
                for s in steps(ph.c):
                    if s[0] == "split_w1":
                        if s[1] == 0:
                            act.wait_ge(experts_loaded, 16 * EXPERT_LOADS)
                        w = slice(s[1] * CH, (s[1] + 1) * CH)
                        nc.scalar.activation(w1_hi[:, w], w1_f[:, w], ACT.Copy).then_inc(w1_hi_done, 1)
                    if s[0] == "up":
                        which, k, t = s[1:]
                        tile = ph.count(lambda o: HSLOT * call(which, k + o) + t)
                        act.wait_ge(up_filled, tile + 1)
                        if HSLOT * call(which, k) + t >= 4:
                            act.wait_ge(down_filled, tile - t % 2 - 2)
                        nc.scalar.activation(hid[:, t % 4, :], up_ps[:, t % 2, :], ACT.Relu,
                                             bias=b1_sb[:, t:t + 1]).then_inc(up_relued, 1)
                    if s[0] == "score_exp":
                        c, h, b = s[1:]
                        act.wait_ge(exp_filled, ph.count(lambda o: 2 * H * (c + o) + 2 * h + b + 1))
                        if h % 4 == 0 and b == 0 and 4 * c + h // 4 >= 2:
                            act.wait_ge(pv_filled, ph.count(lambda o: 4 * (c + o) + h // 4 - 1))
                        nc.scalar.activation(prob[:, h % 8, b, :, :].rearrange("p s n -> p (s n)"),
                                             score_ps[:, b, 0:3 * P], ACT.Exp).then_inc(exp_done, 1)
                    if s[0] == "take_pv":
                        c, g = s[1], s[2]
                        act.wait_ge(pv_filled, ph.count(lambda o: 4 * (c + o) + g + 1))
                        if c >= 1 and g == 0:
                            act.wait_ge(shared_filled, shared_count(ph, ("normalise", c - 1, 3)))
                        nc.scalar.activation(o_t[:, g, :], o_ps[:, :], ACT.Copy).then_inc(o_copied, 1)
                    if s[0] == "transpose_x" and s[1] == 0:
                        k = s[2]
                        act.wait_ge(shared_filled, shared_count(ph, s))
                        if k >= 1:
                            act.wait_ge(xsplit, ph.count(lambda o: 2 * (k + o)))
                        nc.scalar.activation(xt[:, :], shared_ps[:, :], ACT.Copy).then_inc(shared_emptied, 1)
                    if s[0] == "transpose_x" and s[1] > 0:
                        which, k = s[1], s[2]
                        n = call(which, k)
                        act.wait_ge(shared_filled, shared_count(ph, s))
                        if n >= 2:
                            act.wait_ge(up_filled, ph.count(lambda o: HSLOT * (call(which, k + o) - 1)))
                        nc.scalar.activation(xf_hi[:, n % 2, :], shared_ps[:, :], ACT.Copy).then_inc(xf_hi_done, 1)
                    if s[0] == "route":
                        if s[1:] == (1, 0):
                            act.wait_ge(router_loaded, 16 * ROUTER_LOADS)
                        act.wait_ge(shared_filled, shared_count(ph, s))
                        nc.scalar.activation(logit_t[:, :], shared_ps[0:E, :], ACT.Identity, bias=br_sb[:, 0:1])\
                            .then_inc(shared_emptied, 1)
                    if s[0] == "gate":
                        which, k = s[1], s[2]
                        act.wait_ge(gate_step, ph.count(lambda o: GATE_STEPS * call(which, k + o) + 2))
                        nc.scalar.activation(expd[:, :, :], below[:, :, :], ACT.Exp).then_inc(gate_exp, 1)
                    if s[0] == "transpose_g":
                        act.wait_ge(shared_filled, shared_count(ph, s))
                        nc.scalar.activation(gates_t[:, :], shared_ps[0:E, :], ACT.Copy).then_inc(shared_emptied, 1)
                    if s[0] == "project_q":
                        c = s[1]
                        if c == 0:
                            act.wait_ge(rest_loaded, 16 * REST_LOADS)
                        act.wait_ge(shared_filled, shared_count(ph, s))
                        if c >= 1:
                            act.wait_ge(qsplit, ph.count(lambda o: SPLIT_STEPS * (c + o)))
                        nc.scalar.activation(q_f[:, :], shared_ps[:, :], ACT.Identity, bias=bqs_sb[:, 0:1],
                                             scale=QSCALE).then_inc(shared_emptied, 1)
                    if s[0] == "project_k":
                        c = s[1]
                        act.wait_ge(shared_filled, shared_count(ph, s))
                        if c >= 1:
                            act.wait_ge(ksplit, ph.count(lambda o: SPLIT_STEPS * (c + o)))
                        nc.scalar.activation(k_f[:, :], shared_ps[:, :], ACT.Identity, bias=bk_sb[:, 0:1])\
                            .then_inc(shared_emptied, 1)
                    if s[0] == "send_max":
                        c, g = s[1:]
                        act.wait_ge(shared_filled, shared_count(ph, s))
                        if c >= 1:
                            act.wait_ge(max_in[g], ph.count(lambda o: 96 * (c + o)))
                        nc.scalar.activation(mx_t[:, g, :], shared_bf[0:3 * H // 2, 0:CH], ACT.Copy)\
                            .then_inc(shared_emptied, 1)
                    if s[0] == "transpose_o":
                        act.wait_ge(shared_filled, shared_count(ph, s))
                        nc.scalar.activation(o_nt[:, :], shared_ps[:, :], ACT.Copy).then_inc(shared_emptied, 1)

            phases(act, body)

        @block.vector
        def _(dve):
            nc.vector.memset(wr_hi[:, :].bitcast(F32), 0.0).then_inc(rows_cleared, 1)
            nc.vector.memset(wr_lo[:, :].bitcast(F32), 0.0).then_inc(rows_cleared, 1)

            def body(ph):
                for s in steps(ph.c):
                    if s[0] == "split_router":
                        dve.wait_ge(router_loaded, 16 * ROUTER_LOADS)
                        dve.wait_ge(rows_cleared, 2)
                        nc.vector.tensor_copy(wr_hi[:, 0:E], wr_f[:, :]).then_inc(router_split, 1)
                        dve.wait_ge(router_split, 1)
                        nc.vector.tensor_tensor(wr_lo[:, 0:E], wr_f[:, :], wr_hi[:, 0:E].bitcast(F32), ALU.subtract)\
                            .then_inc(router_split, 1)
                    if s[0] == "split_w1":
                        n = s[1]
                        w = slice(n * CH, (n + 1) * CH)
                        dve.wait_ge(w1_hi_done, n + 1)
                        nc.vector.tensor_tensor(w1_lo[:, w], w1_f[:, w], w1_hi[:, w].bitcast(F32), ALU.subtract)\
                            .then_inc(w1_split, 1)
                    if s[0] == "split_qk":
                        dve.wait_ge(rest_loaded, 16 * REST_LOADS)
                        nc.vector.tensor_copy(wqk_hi[:, :, :], wqk_f[:, :, :]).then_inc(qk_split, 1)
                        nc.vector.tensor_scalar(bqs_sb[:, :], bq_sb[:, :], QSCALE, None, ALU.mult).then_inc(qk_split, 1)
                        dve.wait_ge(qk_split, 1)
                        nc.vector.tensor_tensor(wqk_lo[:, :, :], wqk_f[:, :, :], wqk_hi[:, :, :].bitcast(F32),
                                                ALU.subtract).then_inc(qk_split, 1)
                    if s[0] == "down":
                        which, k, t, part = s[1:]
                        if part == 0:
                            continue
                        e, half = t // 2, t % 2
                        n = call(which, k)
                        acc = x1 if which == 1 else y_out
                        at = ph.count(lambda o: HSLOT * call(which, k + o) + t)
                        dve.wait_ge(down_filled, at + 1)
                        if e >= 1:
                            dve.wait_ge(down_added, at - 1)
                        elif half == 0:
                            dve.wait_ge(shared_emptied, shared_count(ph, ("bias_down", which, k)))
                        for tt in (2 * half, 2 * half + 1):
                            last = nc.vector.scalar_tensor_tensor(
                                out=acc[:, k % 2, tt, :], in0=down_ps[:, half, tt % 2, :],
                                scalar=gates[:, n % 2, tt, e:e + 1], in1=acc[:, k % 2, tt, :],
                                op0=ALU.mult, op1=ALU.add)
                        last.then_inc(down_added, 1)
                    if s[0] == "ln_stats":
                        which, k = s[1], s[2]
                        m = min(which, 1)
                        src = (x1, x_in, x2)[which]
                        if which == 0:
                            dve.wait_ge(down_added, ph.count(lambda o: 16 * call_ff1(k + o) + 16))
                        elif which == 1:
                            dve.wait_ge(x_loaded[k % 2], ph.count(lambda o: 16 * ((k + o) // 2 + 1)))
                        else:
                            dve.wait_ge(shared_emptied, shared_count(ph, ("project_o", k)))
                        for tt in range(TT):
                            nc.vector.bn_stats(stats[:, m, tt, :], src[:, k % 2, tt, :]).then_inc(stats_done[m], 1)
                        dve.wait_ge(stats_done[m], ln_count(ph, which, k, TT) + TT)
                        first = k == 0 and which < 2
                        if not first:
                            dve.wait_ge(rstd_done[m], ln_count(ph, which, k, 1))
                        hold(dve)
                        for tt in range(TT):
                            nc.vector.bn_aggr(mv[:, m, tt, :], stats[:, m, tt, :]).then_inc(moments_done[m], 1)
                    if s[0] == "ln_apply":
                        which, k = s[1], s[2]
                        m = min(which, 1)
                        src = (x1, x_in, x2)[which]
                        dve.wait_ge(rstd_done[m], ln_count(ph, which, k, 1) + 1)
                        dve.wait_ge(moments_done[m], ln_count(ph, which, k, TT) + TT)
                        if which == 0 and k >= 1:
                            dve.wait_ge(shared_filled, shared_count(ph, ("transpose_x", 0, k - 1)))
                        elif which == 2 or which == 1 and k >= 1:
                            dve.wait_ge(xf_hi_done, ph.count(lambda o: call(which, k + o)))
                        for tt in range(TT):
                            nc.vector.tensor_scalar(xn[:, m, tt, :], src[:, k % 2, tt, :], mv[:, m, tt, 0:1],
                                                    rstd[:, m, tt:tt + 1], ALU.subtract, ALU.mult)\
                                .then_inc(xn_done[m], 1)
                    if s[0] == "transpose_x" and s[1] == 0:
                        k = s[2]
                        dve.wait_ge(shared_emptied, shared_count(ph, s))
                        if k >= 1:
                            dve.wait_ge(shared_filled, shared_count(ph, ("project_k", k - 1)))
                        nc.vector.tensor_copy(xa_hi[:, :], xt[:, :]).then_inc(xsplit, 1)
                        dve.wait_ge(xsplit, ph.count(lambda o: 2 * (k + o) + 1))
                        nc.vector.tensor_tensor(xa_lo[:, :], xt[:, :], xa_hi[:, :].bitcast(F32), ALU.subtract)\
                            .then_inc(xsplit, 1)
                    if s[0] == "transpose_x" and s[1] > 0:
                        which, k = s[1], s[2]
                        n = call(which, k)
                        dve.wait_ge(xf_hi_done, ph.count(lambda o: call(which, k + o) + 1))
                        nc.vector.tensor_tensor(xf_lo[:, n % 2, :], shared_ps[:, :], xf_hi[:, n % 2, :].bitcast(F32),
                                                ALU.subtract).then_inc(shared_emptied, 1)
                    if s[0] == "gate":
                        which, k = s[1], s[2]
                        n = call(which, k)

                        def step(j):
                            dve.wait_ge(gate_step, ph.count(lambda o: GATE_STEPS * call(which, k + o) + j))

                        dve.wait_ge(shared_filled, shared_count(ph, s))
                        if n >= 1:
                            dve.wait_ge(gate_exp, ph.count(lambda o: call(which, k + o)))
                        nc.vector.tensor_copy(logit[:, :, :], shared_ps[:, 0:TT * E].rearrange("p (t e) -> p t e", e=E))\
                            .then_inc(shared_emptied, 1)
                        dve.wait_ge(shared_emptied, shared_count(ph, s))
                        nc.vector.tensor_reduce(out=top[:, :], in_=logit[:, :, :], op=ALU.max, axis=AX.X)\
                            .then_inc(gate_step, 1)
                        step(1)
                        nc.vector.tensor_tensor(below[:, :, :], logit[:, :, :],
                                                top[:, :].unsqueeze(2).broadcast_to([P, TT, E]), ALU.subtract)\
                            .then_inc(gate_step, 1)
                        other = logit[:, :, :].unsqueeze(2).broadcast_to([P, TT, E, E])
                        own = logit[:, :, :].unsqueeze(3).broadcast_to([P, TT, E, E])
                        nc.vector.tensor_tensor(beats[:, :, :, :], other, own, ALU.is_gt).then_inc(gate_step, 1)
                        nc.vector.tensor_tensor(ties[:, :, :, :], other, own, ALU.is_equal).then_inc(gate_step, 1)
                        step(4)
                        nc.vector.tensor_tensor(ties[:, :, :, :], ties[:, :, :, :],
                                                tri_sb[:, :, :].unsqueeze(1).broadcast_to([P, TT, E, E]), ALU.mult)\
                            .then_inc(gate_step, 1)
                    if s[0] == "gate_end":
                        which, k = s[1], s[2]
                        n = call(which, k)

                        def step(j):
                            dve.wait_ge(gate_step, ph.count(lambda o: GATE_STEPS * call(which, k + o) + j))

                        step(5)
                        nc.vector.tensor_tensor(beats[:, :, :, :], beats[:, :, :, :], ties[:, :, :, :], ALU.add)\
                            .then_inc(gate_step, 1)
                        step(6)
                        nc.vector.tensor_reduce(out=rank[:, :, :], in_=beats[:, :, :, :], op=ALU.add, axis=AX.X)\
                            .then_inc(gate_step, 1)
                        step(7)
                        dve.wait_ge(gate_exp, ph.count(lambda o: call(which, k + o) + 1))
                        nc.vector.scalar_tensor_tensor(out=chosen[:, :, :], in0=rank[:, :, :], scalar=1.5,
                                                       in1=expd[:, :, :], op0=ALU.is_lt, op1=ALU.mult)\
                            .then_inc(gate_step, 1)
                        step(8)
                        nc.vector.tensor_reduce(out=gsum[:, :], in_=chosen[:, :, :], op=ALU.add, axis=AX.X)\
                            .then_inc(gate_step, 1)
                        step(9)
                        nc.vector.reciprocal(grec[:, :], gsum[:, :]).then_inc(gate_step, 1)
                        step(10)
                        nc.vector.scalar_tensor_tensor(out=gates[:, n % 2, :, :], in0=chosen[:, :, :], scalar=0.5,
                                                       in1=grec[:, :].unsqueeze(2).broadcast_to([P, TT, E]),
                                                       op0=ALU.mult, op1=ALU.mult).then_inc(gates_done, 1)
                    if s[0] == "bias_down":
                        which, k = s[1], s[2]
                        res, acc = (x_in, x1) if which == 1 else (x2, y_out)
                        dve.wait_ge(shared_filled, shared_count(ph, s))
                        if which == 1 and k >= 2:
                            dve.wait_ge(x2_seeded, ph.count(lambda o: k + o - 1))
                        if which == 2 and k >= 2:
                            dve.wait_ge(out_stored[k % 2], ph.count(lambda o: 16 * ((k + o) // 2)))
                        nc.vector.tensor_tensor(acc[:, k % 2, :, :],
                                                shared_ps[:, :].rearrange("p (t d) -> p t d", d=D),
                                                res[:, k % 2, :, :], ALU.add).then_inc(shared_emptied, 1)
                    if s[0] == "project_q":
                        c = s[1]

                        def step(j):
                            dve.wait_ge(qsplit, ph.count(lambda o: SPLIT_STEPS * (c + o) + j))

                        dve.wait_ge(shared_emptied, shared_count(ph, s))
                        if c >= 1:
                            dve.wait_ge(qk_out, ph.count(lambda o: 96 * (c + o)))
                        nc.vector.tensor_copy(q_part[:, 0, :], q_f[:, :]).then_inc(qsplit, 1)
                        step(1)
                        nc.vector.tensor_tensor(q_rest[:, :], q_f[:, :], q_part[:, 0, :], ALU.subtract)\
                            .then_inc(qsplit, 1)
                        step(2)
                        nc.vector.tensor_copy(q_part[:, 1, :], q_rest[:, :]).then_inc(qsplit, 1)
                        step(3)
                        nc.vector.tensor_tensor(q_part[:, 2, :], q_rest[:, :], q_part[:, 1, :], ALU.subtract)\
                            .then_inc(qsplit, 1)
                    if s[0] == "project_v":
                        c = s[1]
                        dve.wait_ge(shared_filled, shared_count(ph, s))
                        if c == 0:
                            dve.wait_ge(cleared, 2)
                        if c >= 2:
                            dve.wait_ge(pv_filled, ph.count(lambda o: 4 * (c + o - 1)))
                        for tt in range(TT):
                            last = nc.vector.tensor_tensor(
                                v_st[c % 2][:, tt, :, 0:HD],
                                shared_ps[:, tt * D:(tt + 1) * D].rearrange("p (h d) -> p h d", d=HD),
                                bv_bc[:, :].rearrange("p (h d) -> p h d", d=HD), ALU.add)
                        last.then_inc(shared_emptied, 1)
                    if s[0] == "score_max":
                        c, h, b = s[1:]
                        dve.wait_ge(max_filled, ph.count(lambda o: 2 * H * (c + o) + 2 * h + b + 1))
                        if c >= 1 and h == 0 and b == 0:
                            dve.wait_ge(max_step, ph.count(lambda o: MAX_STEPS * (c + o - 1) + MAX_STEPS // 2 + 1))
                        if c + h >= 1:
                            dve.wait_ge(max_taken, ph.count(lambda o: 2 * H * (c + o) + 2 * h + b - 1))
                        hold(dve)
                        for i, cols in ((0, slice(0, P)), (1, slice(P, 3 * P))):
                            width = cols.stop - cols.start
                            last = nc.vector.tensor_tensor_reduce(
                                out=score_junk[:, b, cols], in0=max_bank(h, b)[:, cols], in1=mask_sb[:, 2 * P - width:],
                                scale=1.0, scalar=-3e38, op0=ALU.add, op1=ALU.max,
                                accum_out=mx[:, 2 * b + i, h:h + 1])
                        last.then_inc(max_taken, 1)
                    if s[0] == "split_max":
                        c, g = s[1:]

                        def step(j):
                            dve.wait_ge(max_step, ph.count(lambda o: MAX_STEPS * (c + o) + MAX_STEPS // 2 * g + j))

                        dve.wait_ge(max_taken, ph.count(lambda o: 2 * H * (c + o) + H * (g + 1)))
                        flat = neg_mx[:, :, g, :, :].rearrange("p t a h -> p t (a h)")
                        rest = mx_rest[:, g, :, :]
                        nc.vector.tensor_scalar(neg_mx[:, :, g, :, :],
                                                mx[:, :, g * H // 2:(g + 1) * H // 2].rearrange(
                                                    "p t (h a) -> p t a h", a=2), -1.0, None,
                                                ALU.mult).then_inc(max_step, 1)
                        step(1)
                        if c >= 1:
                            dve.wait_ge(shared_filled, shared_count(ph, ("send_max", c - 1, g)))
                        nc.vector.tensor_copy(mx_part[:, :, g, 0, :], flat).then_inc(max_step, 1)
                        step(2)
                        nc.vector.tensor_tensor(rest, flat, mx_part[:, :, g, 0, :], ALU.subtract).then_inc(max_step, 1)
                        step(3)
                        nc.vector.tensor_copy(mx_part[:, :, g, 1, :], rest).then_inc(max_step, 1)
                        step(4)
                        nc.vector.tensor_tensor(mx_part[:, :, g, 2, :], rest, mx_part[:, :, g, 1, :], ALU.subtract)\
                            .then_inc(max_step, 1)
                    if s[0] == "normalise":
                        c, tt = s[1], s[2]
                        dve.wait_ge(shared_filled, shared_count(ph, s))
                        if tt == 0 and c >= 1:
                            dve.wait_ge(shared_filled, shared_count(ph, ("transpose_o", c - 1)))
                        o = shared_ps[:, :].rearrange("p (h w) -> p h w", w=32)
                        nc.vector.reciprocal(o_rec[:, :].unsqueeze(2), o[:, :, HD:HD + 1]).then_inc(rec_done, 1)
                        dve.wait_ge(rec_done, ph.count(lambda q: TT * (c + q) + tt + 1))
                        nc.vector.tensor_tensor(o_n[:, tt, :].rearrange("p (h d) -> p h d", d=HD), o[:, :, 0:HD],
                                                o_rec[:, :].unsqueeze(2).broadcast_to([P, H, HD]), ALU.mult)\
                            .then_inc(shared_emptied, 1)
                    if s[0] == "project_o":
                        c = s[1]
                        dve.wait_ge(shared_filled, shared_count(ph, s))
                        dve.wait_ge(x2_seeded, ph.count(lambda o: c + o + 1))
                        nc.vector.tensor_tensor(x2[:, c % 2, :, :], shared_ps[:, :].rearrange("p (t d) -> p t d", d=D),
                                                x2[:, c % 2, :, :], ALU.add).then_inc(shared_emptied, 1)

            phases(dve, body)

        @block.tensor
        def _(pe):
            pe.wait_ge(router_loaded, 16 * ROUTER_LOADS)
            mm, tr = nc.tensor.matmul, nc.tensor.transpose

            def three(out, hi, lo, x_hi, x_lo):
                mm(out, hi, x_hi, start=True, stop=False)
                mm(out, hi, x_lo, start=False, stop=False)
                return mm(out, lo, x_hi, start=False, stop=True)

            def body(ph):
                for s in steps(ph.c):
                    if s[0] in SHARED and SHARED_AT[s] > 0:
                        pe.wait_ge(shared_emptied, shared_count(ph, s) - 1)
                    if s[0] == "up":
                        which, k, t = s[1:]
                        n = call(which, k)
                        tile = ph.count(lambda o: HSLOT * call(which, k + o) + t)
                        if n == 0:
                            pe.wait_ge(w1_split, t // 4 + 1)
                        if n == 0 and t == 0:
                            pe.wait_ge(experts_loaded, 16 * EXPERT_LOADS)
                        if t == 0:
                            pe.wait_ge(shared_emptied, shared_count(ph, ("transpose_x", which, k)))
                        if HSLOT * n + t >= 2:
                            pe.wait_ge(up_relued, tile - 1)
                        w = slice(t * P, (t + 1) * P)
                        three(up_ps[:, t % 2, :], w1_hi[:, w], w1_lo[:, w], xf_hi[:, n % 2, :], xf_lo[:, n % 2, :])\
                            .then_inc(up_filled, 1)
                    if s[0] == "down":
                        which, k, t, part = s[1:]
                        e, half = t // 2, t % 2
                        at = ph.count(lambda o: HSLOT * call(which, k + o) + t)
                        if half == 0 and part == 0:
                            pe.wait_ge(up_relued, at + 2)
                        if part == 0 and HSLOT * call(which, k) + t >= 2:
                            pe.wait_ge(down_added, at - 1)
                        for tt in (2 * half + part,):
                            for j in range(2):
                                last = mm(down_ps[:, half, tt % 2, :], hid[:, (2 * e + j) % 4, tt * P:(tt + 1) * P],
                                          w2_sb[:, e, j, :], start=j == 0, stop=j == 1)
                        if part == 1:
                            last.then_inc(down_filled, 1)
                    if s[0] == "transpose_x":
                        which, k = s[1], s[2]
                        m = min(which, 1)
                        pe.wait_ge(xn_done[m], ln_count(ph, which, k, TT) + TT)
                        for tt in range(TT):
                            last = tr(shared_ps[:, tt * P:(tt + 1) * P], xn[:, m, tt, :], id_f[:, :])
                        last.then_inc(shared_filled, 1)
                    if s[0] == "route":
                        n = call(s[1], s[2])
                        if n == 0:
                            pe.wait_ge(router_split, 2)
                        three(shared_ps[:, :], wr_hi[:, :], wr_lo[:, :], xf_hi[:, n % 2, :], xf_lo[:, n % 2, :])\
                            .then_inc(shared_filled, 1)
                    if s[0] == "gate":
                        hold(pe)
                        for tt in range(TT):
                            last = tr(shared_ps[:, tt * E:(tt + 1) * E], logit_t[:, tt * P:(tt + 1) * P],
                                      id_f[0:E, 0:E])
                        last.then_inc(shared_filled, 1)
                    if s[0] == "transpose_g":
                        which, k = s[1], s[2]
                        n = call(which, k)
                        pe.wait_ge(gates_done, ph.count(lambda o: call(which, k + o) + 1))
                        hold(pe)
                        for tt in range(TT):
                            last = tr(shared_ps[0:E, tt * P:(tt + 1) * P], gates[:, n % 2, tt, :], id_f[:, :])
                        last.then_inc(shared_filled, 1)
                    if s[0] == "bias_down":
                        for tt in range(TT):
                            last = mm(shared_ps[:, tt * D:(tt + 1) * D], gates_t[:, tt * P:(tt + 1) * P], b2_sb[:, :],
                                      start=True, stop=True)
                        last.then_inc(shared_filled, 1)
                    if s[0] in ("project_q", "project_k"):
                        c, j = s[1], int(s[0] == "project_k")
                        if c == 0 and j == 0:
                            pe.wait_ge(qk_split, 3)
                            pe.wait_ge(rest_loaded, 16 * REST_LOADS)
                        pe.wait_ge(xsplit, ph.count(lambda o: 2 * (c + o) + 2))
                        three(shared_ps[:, :], wqk_hi[:, j, :], wqk_lo[:, j, :], xa_hi[:, :], xa_lo[:, :])\
                            .then_inc(shared_filled, 1)
                    if s[0] == "project_v":
                        for tt in range(TT):
                            last = mm(shared_ps[:, tt * D:(tt + 1) * D], xt[:, tt * P:(tt + 1) * P], wv_sb[:, :],
                                      start=True, stop=True)
                        last.then_inc(shared_filled, 1)
                    if s[0] == "score_max":
                        c, h, b = s[1:]
                        if h == 0:
                            if b == 0:
                                pe.wait_ge(qk_in, ph.count(lambda o: 64 * (c + o + 1)))
                            if c >= 1:
                                pe.wait_ge(exp_done, ph.count(lambda o: 2 * H * (c + o) - 1 + b))
                        elif h == 3 and b == 0:
                            if c >= 1:
                                pe.wait_ge(o_copied, ph.count(lambda o: 4 * (c + o)))
                        else:
                            u = 2 * h + b
                            pe.wait_ge(max_taken, ph.count(lambda o: 2 * H * (c + o) + u - (1 if u < 6 else 2)))
                        bank = max_bank(h, b)
                        rows = slice(64 * (h % 2), 64 * (h % 2) + ROWS_A)
                        q, k = q_st[c % 2], k_st[c % 2]
                        for i, cols in ((0, slice(0, P)), (1, slice(P, 3 * P))):
                            i0 = b * T + i * P
                            last = mm(bank[:, cols], q[rows, h // 2, i0:i0 + P],
                                      k[rows, h // 2, b * T:i0 + P], start=True, stop=True)
                        last.then_inc(max_filled, 1)
                    if s[0] == "send_max":
                        c, g = s[1:]
                        pe.wait_ge(max_step, ph.count(lambda o: MAX_STEPS * (c + o) + MAX_STEPS // 2 * (g + 1)))
                        hold(pe)
                        for tt in range(TT):
                            last = tr(shared_bf[0:3 * H // 2, tt * P:(tt + 1) * P], mx_part[:, tt, g, :, :],
                                      id_b[:, :])
                        last.then_inc(shared_filled, 1)
                    if s[0] == "score_exp":
                        c, h, b = s[1:]
                        if h % (H // 2) == 0 and b == 0:
                            pe.wait_ge(max_in[h // (H // 2)], ph.count(lambda o: 96 * (c + o + 1)))
                        if h == 0:
                            if b == 0:
                                pe.wait_ge(max_taken, ph.count(lambda o: 2 * H * (c + o + 1)))
                        else:
                            pe.wait_ge(exp_done, ph.count(lambda o: 2 * H * (c + o) + 2 * h + b - 1))
                        rows = slice(64 * (h % 2), 64 * (h % 2) + ROWS_B)
                        q, k = q_st[c % 2], k_st[c % 2]
                        for j, cols in ((1, slice(2 * P, 3 * P)), (0, slice(0, 2 * P))):
                            j0 = b * T + j * P
                            last = mm(score_ps[:, b, cols], k[rows, h // 2, j0:j0 + P],
                                      q[rows, h // 2, j0:(b + 1) * T], start=True, stop=True)
                        last.then_inc(exp_filled, 1)
                    if s[0] == "pv":
                        c, g = s[1], s[2]
                        pe.wait_ge(causal_done, ph.count(lambda o: 2 * H * (c + o) + 8 * g + 8))
                        if 4 * c + g >= 1:
                            pe.wait_ge(o_copied, ph.count(lambda o: 4 * (c + o) + g))
                        for b in range(2):
                            for j in range(2):
                                for hh in range(4):
                                    h = 4 * g + hh
                                    p = prob[:, h % 8, b, 0:2, :] if j == 0 else prob[:, h % 8, b, 2:3, :]
                                    last = mm(o_ps[32 * hh:32 * hh + 32, b * T + j * P:(b + 1) * T],
                                              v_st[c % 2][:, 2 * b + j, h, :], p, start=j == 0, stop=j == 1)
                        last.then_inc(pv_filled, 1)
                    if s[0] == "normalise":
                        c, tt = s[1], s[2]
                        if tt == 0:
                            pe.wait_ge(o_copied, ph.count(lambda o: 4 * (c + o) + 4))
                        for g in range(4):
                            last = tr(shared_ps[:, g * P:(g + 1) * P], o_t[:, g, tt * P:(tt + 1) * P], id_f[:, :])
                        last.then_inc(shared_filled, 1)
                    if s[0] == "transpose_o":
                        for tt in range(TT):
                            last = tr(shared_ps[:, tt * P:(tt + 1) * P], o_n[:, tt, :], id_f[:, :])
                        last.then_inc(shared_filled, 1)
                    if s[0] == "project_o":
                        for tt in range(TT):
                            last = mm(shared_ps[:, tt * D:(tt + 1) * D], o_nt[:, tt * P:(tt + 1) * P], wo_sb[:, :],
                                      start=True, stop=True)
                        last.then_inc(shared_filled, 1)

            phases(pe, body)


def kernel(L0_attn_x, L0_attn_Wq, L0_attn_bq, L0_attn_Wk, L0_attn_bk, L0_attn_Wv, L0_attn_bv, L0_attn_Wo,
           L0_attn_bo, L0_ffn_Wr, L0_ffn_br, L0_ffn_W1, L0_ffn_b1, L0_ffn_W2, L0_ffn_b2):
    import numpy as np
    import ml_dtypes
    import concourse.bacc as bacc
    from concourse.bass_utils import run_bass_kernel_spmd

    lay = np.ascontiguousarray
    a = {
        "x": lay(np.asarray(L0_attn_x).reshape(B * T, D)),
        "wq": lay(np.asarray(L0_attn_Wq).T), "bq": lay(np.asarray(L0_attn_bq).reshape(D, 1)),
        "wk": lay(np.asarray(L0_attn_Wk).T), "bk": lay(np.asarray(L0_attn_bk).reshape(D, 1)),
        "wv": lay(np.asarray(L0_attn_Wv).T), "bv": lay(np.asarray(L0_attn_bv)),
        "wo": lay(np.asarray(L0_attn_Wo).T), "bo": lay(np.asarray(L0_attn_bo)),
        "wr": lay(np.asarray(L0_ffn_Wr)), "br": lay(np.asarray(L0_ffn_br).reshape(E, 1)),
        "w1": lay(np.asarray(L0_ffn_W1).transpose(1, 0, 2).reshape(D, E * HID)),
        "b1": lay(np.asarray(L0_ffn_b1).reshape(E * 2, P).T),
        "w2": lay(np.asarray(L0_ffn_W2).reshape(E, 2, P, D).transpose(2, 0, 1, 3)),
        "b2": lay(np.asarray(L0_ffn_b2)),
    }
    bf = ml_dtypes.bfloat16
    a["ident"] = np.eye(P, dtype=np.float32)
    a["ident_b"] = np.eye(P, dtype=bf)
    a["mask"] = np.concatenate([np.zeros((P, P), np.float32), np.triu(np.full((P, P), -1e30, np.float32), 1)], 1)
    a["tri"] = np.tril(np.ones((E, E), np.float32), -1).reshape(E * E)
    pos = np.tile(np.arange(T, dtype=np.float32), 2)
    rows_q = np.zeros((64 - ROWS_QK, H // 2, CH), np.float32)
    rows_k = np.zeros((64 - ROWS_QK, H // 2, CH), np.float32)
    rows_q[0], rows_q[1] = 1.0, -pos
    rows_k[0], rows_k[1:5] = pos, 1.0
    masks = [(block * P + first, length) for block in range(2) for first, length in MASKED]
    for r, (first, length) in enumerate(masks, ROWS_M - ROWS_QK):
        rows_q[r] = (pos >= first) & (pos < first + length // 2)
        rows_k[r] = np.where((pos >= first + length // 2) & (pos < first + length), -1e30, 0.0)
    a["qrows"], a["krows"] = rows_q.astype(bf), rows_k.astype(bf)

    nc = bacc.Bacc("TRN2", target_bir_lowering=False, num_devices=1)
    arrays, args = {}, []
    for name, arr in a.items():
        arrays[name + "_dram"] = arr
        args.append(nc.dram_tensor(name + "_dram", arr.shape, mybir.dt.from_np(arr.dtype), kind="ExternalInput").ap())
    for name in ("zq", "zk"):
        args.append(nc.dram_tensor(name, [2, P, PIECES, CH], BF16, kind="Internal").ap())
    args.append(nc.dram_tensor("out_dram", [B * T, D], F32, kind="ExternalOutput").ap())
    macaron_kernel(nc, *args)
    r = run_bass_kernel_spmd(nc, [arrays], core_ids=[0])
    return r.results[0]["out_dram"].reshape(B, T, D)
```
